# Optimizing a Trainium2 kernel written in Bass

```python
import numpy as np
import jax
import jax.numpy as jnp

def _softmax(x, axis=-1):
    return jax.nn.softmax(x, axis=axis)

def _gelu(x):
    return jax.nn.gelu(x, approximate=True)

def _silu(x):
    return jax.nn.silu(x)

def _sigmoid(x):
    return jax.nn.sigmoid(x)

def _layernorm(x, axis=-1, eps=1e-05):
    m = jnp.mean(x, axis=axis, keepdims=True)
    v = jnp.var(x, axis=axis, keepdims=True)
    return (x - m) / jnp.sqrt(v + eps)

def _scatter_add(tgt, idx, src, axis=0):
    return tgt.at[idx].add(src)

def _segment_sum(src, seg, n):
    return jax.ops.segment_sum(src, seg, n)
kernel_name = 'mk_conv_preact_d2_conv_nchw64_r2_ae7098'

def setup_inputs(seed: int=0):
    np.random.seed(seed)
    _w = jnp.asarray

    def _rec_inputs():
        import jax
        import jax.numpy as jnp
        _gk = jax.random.key(seed)
        x = -0.0001329 + 0.9999 * jax.random.normal(jax.random.fold_in(_gk, 1), (32, 32, 96, 96), jnp.float32)
        return x
    x = _rec_inputs()

    def _L0_conv_setup():
        import jax, jax.numpy as jnp
        import numpy as np
        from jax import lax
        E, K = (6, 3)

        def _dwconv(x, w, b):
            y = lax.conv_general_dilated(x, w, window_strides=(1, 1), padding=[(1, 1), (1, 1)], dimension_numbers=('NCHW', 'OIHW', 'NCHW'), feature_group_count=w.shape[0])
            return y + b[None, :, None, None]

        def _gate(x, fc0_w, fc0_b, fc1_w, fc1_b):
            pooled = jnp.max(x, axis=(2, 3)) + jnp.mean(x, axis=(2, 3))
            g = jax.nn.leaky_relu(pooled @ fc1_w.T + fc1_b, 0.2)
            noise = jax.nn.softplus(pooled @ fc0_w.T + fc0_b)
            nz = (noise - noise.mean(axis=1, keepdims=True)) / jnp.std(noise, axis=1, ddof=1, keepdims=True)
            _, idx = lax.top_k(g + nz, K)
            b_rows = jnp.arange(g.shape[0])[:, None]
            mask = jnp.zeros_like(g).at[b_rows, idx].set(1.0)
            logits = jnp.where(mask > 0, g, -jnp.inf)
            return jax.nn.softmax(logits, axis=1)
        key = jax.random.key(seed)
        ks = jax.random.split(key, 9)
        B, C, H, W = (32, 32, 96, 96)
        return {'x': jax.random.normal(ks[0], (B, C, H, W), jnp.float32), 'fc0_w': jax.random.normal(ks[1], (E, C), jnp.float32) * 0.1, 'fc0_b': jax.random.normal(ks[2], (E,), jnp.float32) * 0.1, 'fc1_w': jax.random.normal(ks[3], (E, C), jnp.float32) * 0.1, 'fc1_b': jax.random.normal(ks[4], (E,), jnp.float32) * 0.1, 'w1': jax.random.normal(ks[5], (E, C, 1, 3, 3), jnp.float32) * 0.1, 'b1': jax.random.normal(ks[6], (E, C), jnp.float32) * 0.1, 'w2': jax.random.normal(ks[7], (E, C, 1, 3, 3), jnp.float32) * 0.1, 'b2': jax.random.normal(ks[8], (E, C), jnp.float32) * 0.1}
    _L0_conv_all = _L0_conv_setup()
    _L0_conv_in = {k: v for k, v in _L0_conv_all.items() if k in ('fc0_w', 'fc0_b', 'fc1_w', 'fc1_b', 'w1', 'b1', 'w2', 'b2')}
    del _L0_conv_all

    def _L1_conv_setup():
        import jax, jax.numpy as jnp
        import numpy as np
        P = 8

        def _forward(x, w_in, dw_k, fft_filter, w_out):
            b, c, H, W = x.shape
            x = jnp.einsum('oc,bchw->bohw', w_in, x)
            C2 = x.shape[1]
            xp = x.reshape(b, C2, H // P, P, W // P, P).transpose(0, 1, 2, 4, 3, 5)
            xf = jnp.fft.rfft2(xp.astype(jnp.float32)) * fft_filter
            xp = jnp.fft.irfft2(xf, s=(P, P))
            x = xp.transpose(0, 1, 2, 4, 3, 5).reshape(b, C2, H, W)
            y = jax.lax.conv_general_dilated(x, dw_k, window_strides=(1, 1), padding='SAME', dimension_numbers=('NCHW', 'OIHW', 'NCHW'), feature_group_count=C2)
            hid = C2 // 2
            x1, x2 = (y[:, :hid], y[:, hid:])
            g = jax.nn.gelu(x1, approximate=False) * x2
            return jnp.einsum('oc,bchw->bohw', w_out, g)
        key = jax.random.key(seed)
        k1, k2, k3, k4 = jax.random.split(key, 4)
        dim, hidden = (32, 85)
        h2 = hidden * 2
        x = jax.random.normal(k1, (4, dim, 128, 128), dtype=jnp.float32)
        w_in = jax.random.normal(k2, (h2, dim), dtype=jnp.float32) * 0.02
        dw_k = jax.random.normal(k3, (h2, 1, 3, 3), dtype=jnp.float32) * 0.02
        fft_filter = jnp.ones((h2, 1, 1, P, P // 2 + 1), dtype=jnp.float32)
        w_out = jax.random.normal(k4, (dim, hidden), dtype=jnp.float32) * 0.02
        return {'x': x, 'w_in': w_in, 'dw_k': dw_k, 'fft_filter': fft_filter, 'w_out': w_out}
    _L1_conv_all = _L1_conv_setup()
    _L1_conv_in = {k: v for k, v in _L1_conv_all.items() if k in ('w_in', 'dw_k', 'fft_filter', 'w_out')}
    del _L1_conv_all
    return {'x': x, 'L0_conv_fc0_w': _L0_conv_in['fc0_w'], 'L0_conv_fc0_b': _L0_conv_in['fc0_b'], 'L0_conv_fc1_w': _L0_conv_in['fc1_w'], 'L0_conv_fc1_b': _L0_conv_in['fc1_b'], 'L0_conv_w1': _L0_conv_in['w1'], 'L0_conv_b1': _L0_conv_in['b1'], 'L0_conv_w2': _L0_conv_in['w2'], 'L0_conv_b2': _L0_conv_in['b2'], 'L1_conv_w_in': _L1_conv_in['w_in'], 'L1_conv_dw_k': _L1_conv_in['dw_k'], 'L1_conv_fft_filter': _L1_conv_in['fft_filter'], 'L1_conv_w_out': _L1_conv_in['w_out']}

def reference(x, L0_conv_fc0_w, L0_conv_fc0_b, L0_conv_fc1_w, L0_conv_fc1_b, L0_conv_w1, L0_conv_b1, L0_conv_w2, L0_conv_b2, L1_conv_w_in, L1_conv_dw_k, L1_conv_fft_filter, L1_conv_w_out):
    import jax
    import jax.numpy as jnp

    def _L0_conv_ref(x, fc0_w, fc0_b, fc1_w, fc1_b, w1, b1, w2, b2):
        import jax, jax.numpy as jnp
        import numpy as np
        from jax import lax
        E, K = (6, 3)

        def _dwconv(x, w, b):
            y = lax.conv_general_dilated(x, w, window_strides=(1, 1), padding=[(1, 1), (1, 1)], dimension_numbers=('NCHW', 'OIHW', 'NCHW'), feature_group_count=w.shape[0])
            return y + b[None, :, None, None]

        def _gate(x, fc0_w, fc0_b, fc1_w, fc1_b):
            pooled = jnp.max(x, axis=(2, 3)) + jnp.mean(x, axis=(2, 3))
            g = jax.nn.leaky_relu(pooled @ fc1_w.T + fc1_b, 0.2)
            noise = jax.nn.softplus(pooled @ fc0_w.T + fc0_b)
            nz = (noise - noise.mean(axis=1, keepdims=True)) / jnp.std(noise, axis=1, ddof=1, keepdims=True)
            _, idx = lax.top_k(g + nz, K)
            b_rows = jnp.arange(g.shape[0])[:, None]
            mask = jnp.zeros_like(g).at[b_rows, idx].set(1.0)
            logits = jnp.where(mask > 0, g, -jnp.inf)
            return jax.nn.softmax(logits, axis=1)
        cof = _gate(x, fc0_w, fc0_b, fc1_w, fc1_b)
        out = jnp.zeros_like(x)
        for e in range(E):
            h = _dwconv(x, w1[e], b1[e])
            h = jax.nn.relu(h)
            h = _dwconv(h, w2[e], b2[e])
            out = out + cof[:, e][:, None, None, None] * h
        return out

    def _L1_conv_ref(x, w_in, dw_k, fft_filter, w_out):
        import jax, jax.numpy as jnp
        import numpy as np
        P = 8

        def _forward(x, w_in, dw_k, fft_filter, w_out):
            b, c, H, W = x.shape
            x = jnp.einsum('oc,bchw->bohw', w_in, x)
            C2 = x.shape[1]
            xp = x.reshape(b, C2, H // P, P, W // P, P).transpose(0, 1, 2, 4, 3, 5)
            xf = jnp.fft.rfft2(xp.astype(jnp.float32)) * fft_filter
            xp = jnp.fft.irfft2(xf, s=(P, P))
            x = xp.transpose(0, 1, 2, 4, 3, 5).reshape(b, C2, H, W)
            y = jax.lax.conv_general_dilated(x, dw_k, window_strides=(1, 1), padding='SAME', dimension_numbers=('NCHW', 'OIHW', 'NCHW'), feature_group_count=C2)
            hid = C2 // 2
            x1, x2 = (y[:, :hid], y[:, hid:])
            g = jax.nn.gelu(x1, approximate=False) * x2
            return jnp.einsum('oc,bchw->bohw', w_out, g)
        return _forward(x, w_in, dw_k, fft_filter, w_out)

    def _gn(v, G=32, eps=1e-05):
        B_, C_, H_, W_ = v.shape
        g = v.reshape(B_, G, C_ // G, H_, W_)
        m = jnp.mean(g, axis=(2, 3, 4), keepdims=True)
        s = jnp.var(g, axis=(2, 3, 4), keepdims=True)
        return ((g - m) / jnp.sqrt(s + eps)).reshape(v.shape)

    def _ln_c(v, eps=1e-06):
        m = jnp.mean(v, axis=1, keepdims=True)
        s = jnp.var(v, axis=1, keepdims=True)
        return (v - m) / jnp.sqrt(s + eps)

    def _ln_t(v, eps=1e-05):
        m = jnp.mean(v, axis=-1, keepdims=True)
        s = jnp.var(v, axis=-1, keepdims=True)
        return (v - m) / jnp.sqrt(s + eps)

    def _to_tokens(v):
        B_, C_, H_, W_ = v.shape
        return v.reshape(B_, C_, H_ * W_).transpose(0, 2, 1)

    def _from_tokens(t, like):
        B_, C_, H_, W_ = like.shape
        return t.transpose(0, 2, 1).reshape(B_, C_, H_, W_)
    x = x + _L0_conv_ref(_gn(x), L0_conv_fc0_w, L0_conv_fc0_b, L0_conv_fc1_w, L0_conv_fc1_b, L0_conv_w1, L0_conv_b1, L0_conv_w2, L0_conv_b2)
    x = x + _L1_conv_ref(_gn(x), L1_conv_w_in, L1_conv_dw_k, L1_conv_fft_filter, L1_conv_w_out)
    return x

_drawn_inputs = setup_inputs


def setup_inputs(seed=0):
    import zlib

    import numpy as np

    out = dict(_drawn_inputs(seed))
    spreads = {'L1_conv_fft_filter': (1.0, 0.6)}
    factors = {'L0_conv_fc0_w': 4.745,
     'L0_conv_fc1_b': 8.0,
     'L0_conv_b1': 4.307,
     'L1_conv_w_in': 8.0,
     'L1_conv_dw_k': 8.0,
     'L1_conv_w_out': 8.0}
    for name, (base, spread) in spreads.items():
        noise = np.random.default_rng([zlib.crc32(name.encode()), seed]).standard_normal(out[name].shape)
        drawn = base * np.exp(spread * noise) if base else spread * noise
        out[name] = jnp.asarray(drawn.astype(out[name].dtype))
    for name, factor in factors.items():
        out[name] = (out[name] * factor).astype(out[name].dtype)
    return out
```

```python
from contextlib import ExitStack

import numpy as np

import concourse.bass as bass
from concourse import mybir

F32 = mybir.dt.float32
ALU = mybir.AluOpType
ACT = mybir.ActivationFunctionType
AX = mybir.AxisListType

P = 128
B, C, H, W = 32, 32, 96, 96
E, K = 6, 3
IMG = P // C
G = B // IMG
PX = H * W
WP = W + 2
HP = H + 2
TAPS = [(dy, dx) for dy in range(3) for dx in range(3)]
NT = len(TAPS)
GN_EPS = 1e-5

HID = 85
H2 = 2 * HID
T8 = 8
SR = T8
NS = H // SR
NPAIR = W // (2 * T8)
SPX = SR * W
NF = T8 // 2 + 1


def hartley_pairs():
    m = np.arange(T8)
    a = 2 * np.pi * ((m[:, None, None, None] * m[None, None, :, None]
                      + m[None, :, None, None] * m[None, None, None, :]) % T8) / T8
    cas = np.cos(a) + np.sin(a)
    full = np.zeros((T8, 2, T8, 2, T8, T8))
    for j in range(2):
        full[:, j, :, j] = cas
    return full.reshape(P, P).astype(np.float32)


def filter_spread():
    s = np.zeros((T8, NF, 2, T8, T8))
    for u in range(T8):
        for v in range(T8):
            mu = (-u) % T8
            if v in (0, T8 // 2):
                s[u, v, :, u, v] += 0.5
                s[mu, v, :, u, v] += 0.5
            elif v < T8 // 2:
                s[u, v, :, u, v] = 1.0
            else:
                s[mu, T8 - v, :, u, v] = 1.0
    return s.reshape(T8 * NF, P).astype(np.float32)


CH = 5
R1, R2 = 40, 40
N1, N2 = R1 // CH, R2 // CH
NB1 = 6
BN_ROWS = 4
NBN = H // BN_ROWS

GATE = ["veps", "negm", "rstd", "center", "pool1", "pool2", "pooled", "pmask", "logits", "z", "g", "nabs",
        "exp", "ln", "noise", "nsum", "nmean", "dev", "sq", "ss", "var", "istd", "score", "gt", "eq", "tie",
        "cmp", "rank", "hot", "gp", "gsel", "gmax", "nmax", "cexp", "csum", "crec", "cof", "bcast", "bc",
        "pr0", "pr1", "pr2", "wsel", "w1", "b1", "w2", "cb", "cbs", "bx"]
NG = len(GATE)


def experts_part(nc, x, fc0_w, fc0_b, fc1_w, fc1_b, w1, b1, w2, b2, x1, norm2):
    mask = nc.inline_tensor(np.kron(np.eye(IMG), np.ones((C, 1))).astype(np.float32), name="image_mask")
    mask_t = nc.inline_tensor(np.kron(np.eye(IMG), np.ones((1, C))).astype(np.float32), name="image_mask_t")
    tri_c = nc.inline_tensor(np.tile(np.tril(np.ones((E, E)), -1).reshape(1, E, E), (IMG, 1, 1)).astype(np.float32), name="lower_first")
    slot_c = nc.inline_tensor(np.tile(np.arange(K).reshape(1, K), (IMG, 1)).astype(np.float32), name="slot_numbers")
    eye_c = nc.inline_tensor(np.eye(P, dtype=np.float32), name="eye1")

    xg = x.rearrange("(g b) c h w -> g (b c) h w", b=IMG)
    x1g = x1.ap().rearrange("g p (h w) -> g p h w", h=H)

    with ExitStack() as ctx:
        def sb(name, shape):
            return ctx.enter_context(nc.sbuf_tensor(name, shape, F32))

        def sem(name):
            return ctx.enter_context(nc.semaphore(name))

        X = [sb(f"x_pad{q}", [P, HP, WP]) for q in range(2)]
        Hd = [sb(f"hidden{s}", [P, HP, WP]) for s in range(K)]
        diag = [sb(f"diag{q}", [P, NT, P]) for q in range(2)]
        ident = sb("ident", [P, P])
        wall = sb("wall", [P, E, 20])
        fc = sb("fc", [P, 2 * E])
        fcb = sb("fcb", [IMG, 2 * E])
        m4 = sb("m4", [P, IMG])
        m4t = sb("m4t", [IMG, P])
        tri = sb("tri", [IMG, E, E])
        slots = sb("slots", [IMG, K])
        mhalf = sb("mhalf", [P, 1])
        bn = sb("bn", [P, NBN, 6])
        bn1 = sb("bn1", [P, NBN, 6])
        mv = sb("mv", [P, 2])
        mv1 = sb("mv1", [P, 2])
        col = sb("col", [P, 16])
        v1 = sb("v1", [P, 2])
        st2 = sb("st2", [P, 2])
        row = sb("row", [IMG, 160])
        sq6 = sb("sq6", [IMG, 2, E, E])
        R = sb("R", [IMG, K * E + K])
        bc = sb("bc", [P, K * E + K])
        prod = sb("prod", [P, K, 20, E])
        wsel = sb("wsel", [P, K, 20])
        w1c = [sb(f"w1c{q}", [P, K, NT]) for q in range(2)]
        w2c = [sb(f"w2c{q}", [P, K, NT]) for q in range(2)]
        b1c = [sb(f"b1c{q}", [P, K]) for q in range(2)]
        cb = sb("cb", [P, K + 1])
        bxc = [sb(f"bxc{q}", [P, 1]) for q in range(2)]
        ps = [ctx.enter_context(nc.psum_tensor(f"ps{i}", [P, 512], F32)) for i in range(8)]

        VEPS, NEGM, RSTD, MX, SUMC, P1, P2, PL, PM = 0, 1, 2, 3, 4, 5, 6, 7, 8
        c1 = lambda i, n=1: col[:, i:i + n]
        z, g_, na, ex, ln, noi = (row[:, 12 * i:12 * i + 12] for i in range(6))
        dev, sq, sc, rank = (row[:, 72 + 6 * i:78 + 6 * i] for i in range(4))
        nsum, nmean, ss, var, istd, gmax, nmax, csum, crec = (row[:, 96 + i:97 + i] for i in range(9))
        gsel, cexp = row[:, 106:109], row[:, 110:113]
        gp = row[:, 120:138]

        PE_G = K * N1 + K - 1
        B2_G = NBN + 5
        s_const = sem("const_loaded")
        s_set = sem("buffers_set")
        s_x = [sem(f"x_loaded{q}") for q in range(2)]
        s_st = [sem(f"x1_stored{q}") for q in range(2)]
        s_n2 = sem("norm2_stored")
        s_bns = sem("x_stats")
        s_gate = sem("gate_steps")
        s_pl = sem("gate_logits")
        s_diag = sem("diag_built")
        s_pe = sem("pe_units")
        s_c2 = sem("c2_pe_chunks")
        s_ev = sem("c1_pe_evacuated")
        s_tap0 = sem("c1_tap0")
        s_tap1 = sem("c1_taps")
        s_relu = sem("c1_relu")
        s_xb = sem("x_biased")
        s_tap2 = sem("c2_taps")
        s_add = sem("c2_pe_added")
        s_b2 = sem("x1_stats")

        block = ctx.enter_context(nc.Block())
        inner = lambda t, r0, r1: t[:, 1 + r0:1 + r1, 1:1 + W]
        shifted = lambda t, r0, r1, k: t[:, r0 + TAPS[k][0]:r1 + TAPS[k][0], TAPS[k][1]:TAPS[k][1] + W]
        gate_at = lambda g, name: g * NG + GATE.index(name) + 1
        at = lambda g, per, n: g * per + (per + n)
        NCONST = 5 + 7 * IMG + IMG

        def groups(eng, body):
            with eng.Fori(0, G // 2 - 1) as i:
                for q in range(2):
                    body(i * 2 + q, i, q, True)
            for q in range(2):
                body(G - 2 + q, G // 2 - 1, q, q == 0)

        @block.sync
        def _(sp):
            cdma = lambda o, i: sp.dma_start(o, i).then_inc(s_const, 16)
            for q in range(2):
                sp.sem_inc(s_st[q], 16)
            sp.sem_inc(s_n2, 16)
            sp.wait_ge(s_set, 1)
            for h in range(2):
                sp.dma_start(inner(X[0], 48 * h, 48 * h + 48), xg[0][:, 48 * h:48 * h + 48]).then_inc(s_x[0], 16)
            cdma(m4[:, :], mask.ap())
            cdma(m4t[:, :], mask_t.ap())
            cdma(tri[:, :, :], tri_c.ap())
            cdma(slots[:, :], slot_c.ap())
            cdma(ident[:, :], eye_c.ap())
            with nc.allow_non_contiguous_dma(reason="small weight tables, once"):
                for b in range(IMG):
                    o = slice(C * b, C * b + C)
                    cdma(fc[o, 0:E], fc1_w.rearrange("e c -> c e"))
                    cdma(fc[o, E:2 * E], fc0_w.rearrange("e c -> c e"))
                    cdma(wall[o, :, 0:9], w1.rearrange("e c a h w -> c e (a h w)"))
                    cdma(wall[o, :, 9:18], w2.rearrange("e c a h w -> c e (a h w)"))
                    cdma(wall[o, :, 18], b1.rearrange("e c -> c e"))
                    cdma(wall[o, :, 19], b2.rearrange("e c -> c e"))
                    cdma(fcb[b:b + 1, 0:E], fc1_b.rearrange("(a e) -> a e", a=1))
                    cdma(fcb[b:b + 1, E:2 * E], fc0_b.rearrange("(a e) -> a e", a=1))

            def body(g, i, q, more):
                if more:
                    sp.wait_ge(s_set, 2)
                    sp.wait_ge(s_st[1 - q], i * 16 + (16 + 16 * q))
                    for h in range(2):
                        sp.dma_start(inner(X[1 - q], 48 * h, 48 * h + 48),
                                     xg[g + 1][:, 48 * h:48 * h + 48]).then_inc(s_x[1 - q], 16)
                sp.wait_ge(s_add, at(g, N2, N2))
                sp.wait_ge(s_tap2, at(g, K * NT, K * NT))
                sp.dma_start(x1g[g], inner(X[q], 0, H)).then_inc(s_st[q], 16)
                sp.wait_ge(s_b2, at(g, B2_G, B2_G))
                sp.dma_start(norm2.ap()[g], st2[:, :]).then_inc(s_n2, 16)

            groups(sp, body)
            for q in range(2):
                sp.wait_ge(s_st[q], (G // 2 + 1) * 16)
            sp.wait_ge(s_n2, (G + 1) * 16)

        @block.gpsimd
        def _(pool):
            pool.sem_inc(s_diag, 2 * K)
            nc.gpsimd.memset(X[0][:, :, :], 0.0).then_inc(s_set, 1)
            nc.gpsimd.memset(X[1][:, :, :], 0.0).then_inc(s_set, 1)
            nc.gpsimd.memset(mhalf[:, :], -0.5).then_inc(s_set, 1)
            for s in range(K):
                nc.gpsimd.memset(Hd[s][:, :, :], 0.0).then_inc(s_set, 1)
            pool.wait_ge(s_const, 16 * NCONST)
            pool.wait_ge(s_set, 3)

            def rstd(gi):
                pool.wait_ge(s_gate, gate_at(gi, "negm"))
                nc.gpsimd.tensor_tensor(c1(RSTD), c1(VEPS), mhalf[:, :], ALU.pow).then_inc(s_gate, 1)

            def istd_(gi):
                pool.wait_ge(s_gate, gate_at(gi, "var"))
                nc.gpsimd.tensor_tensor(istd, var, mhalf[0:IMG, :], ALU.pow).then_inc(s_gate, 1)

            rstd(0)
            istd_(0)

            def body(g, i, q, more):
                for k in range(2 * K):
                    n = k - 2
                    if n == -2:
                        pool.wait_ge(s_gate, g * NG + NG)
                        pool.wait_ge(s_pe, g * PE_G + PE_G)
                    elif n == -1:
                        pool.wait_ge(s_c2, g * N2 + N2)
                    else:
                        pool.wait_ge(s_pe, at(g, PE_G, (n + 1) * N1 if n < K else K * N1 + n - K + 1))
                    wt = (w1c if k < K else w2c)[q][:, k % K, :]
                    nc.gpsimd.tensor_tensor(diag[k % 2][:, :, :],
                                            ident[:, :].unsqueeze(1).broadcast_to([P, NT, P]),
                                            wt.unsqueeze(2).broadcast_to([P, NT, P]), ALU.mult).then_inc(s_diag, 1)
                    if k == K and more:
                        rstd(g + 1)
                        istd_(g + 1)
                pool.wait_ge(s_b2, at(g, B2_G, NBN + 2))
                nc.gpsimd.tensor_tensor(v1[:, 1:2], v1[:, 0:1], mhalf[:, :], ALU.pow).then_inc(s_b2, 1)

            groups(pool, body)

        @block.scalar
        def _(act):
            act.sem_inc(s_ev, K * N1)
            act.sem_inc(s_tap0, K)
            act.sem_inc(s_relu, K)
            act.sem_inc(s_xb, 1)

            def center(gi, q):
                act.wait_ge(s_gate, gate_at(gi, "rstd"))
                act.wait_ge(s_bns, gi * (NBN + 2) + (NBN + 2))
                nc.scalar.activation(inner(X[q], 0, H), inner(X[q], 0, H), ACT.Identity,
                                     bias=c1(NEGM), accum_out=c1(SUMC)).then_inc(s_gate, 1)

            def gate_noise(gi):
                act.wait_ge(s_gate, gate_at(gi, "nabs"))
                nc.scalar.activation(ex[:, 0:E], na[:, 0:E], ACT.Exp).then_inc(s_gate, 1)
                act.wait_ge(s_gate, gate_at(gi, "exp"))
                nc.scalar.activation(ln[:, 0:E], ex[:, 0:E], ACT.Ln, bias=1.0).then_inc(s_gate, 1)

            def gate_softmax(gi):
                act.wait_ge(s_gate, gate_at(gi, "nmax"))
                nc.scalar.activation(cexp, gsel, ACT.Exp, bias=nmax).then_inc(s_gate, 1)

            act.wait_ge(s_set, 3 + K)
            center(0, 0)
            gate_noise(0)
            gate_softmax(0)

            def body(g, i, q, more):
                act.wait_ge(s_gate, g * NG + NG)
                for s in range(K):
                    act.wait_ge(s_tap2, g * (K * NT) + (s + 1) * NT)
                    if s < K - 1:
                        act.wait_ge(s_pe, g * PE_G + (K * N1 + s + 1))
                    else:
                        act.wait_ge(s_c2, g * N2 + N2)
                    nc.scalar.activation(inner(Hd[s], R1, H), shifted(X[q], R1, H, 0), ACT.Identity,
                                         scale=w1c[q][:, s, 0:1], bias=b1c[q][:, s:s + 1]).then_inc(s_tap0, 1)
                for s in range(K):
                    for n in range(N1):
                        u = s * N1 + n
                        act.wait_ge(s_pe, at(g, PE_G, u + 1))
                        nc.scalar.activation(inner(Hd[s], n * CH, n * CH + CH),
                                             ps[u % NB1][:, 0:CH * W].rearrange("p (h w) -> p h w", h=CH),
                                             ACT.Relu, bias=b1c[q][:, s:s + 1]).then_inc(s_ev, 1)
                        if more and (s, n) == (2, 1):
                            center(g + 1, 1 - q)
                        if more and (s, n) == (2, 4):
                            gate_noise(g + 1)
                            gate_softmax(g + 1)
                    act.wait_ge(s_tap1, at(g, K * (NT - 1), (s + 1) * (NT - 1)))
                    if s == K - 1:
                        nc.scalar.activation(inner(X[q], R2, H), inner(X[q], R2, H), ACT.Identity,
                                             bias=bxc[q][:, :]).then_inc(s_xb, 1)
                    nc.scalar.activation(inner(Hd[s], R1, H), inner(Hd[s], R1, H), ACT.Relu).then_inc(s_relu, 1)

            groups(act, body)

        @block.tensor
        def _(pe):
            pe.sem_inc(s_pe, PE_G)
            pe.sem_inc(s_c2, N2)

            def logits(gi):
                pe.wait_ge(s_gate, gate_at(gi, "pmask"))
                nc.tensor.matmul(ps[7][0:IMG, 0:2 * E], c1(PM, IMG), fc[:, :], start=True, stop=True).then_inc(s_gate, 1)

            def spread(gi):
                pe.wait_ge(s_gate, gate_at(gi, "cof"))
                nc.tensor.matmul(ps[7][:, 0:K * E + K], m4t[:, :], R[:, :], start=True, stop=True).then_inc(s_gate, 1)

            pe.wait_ge(s_const, 16 * NCONST)
            logits(0)
            spread(0)

            def body(g, i, q, more):
                for s in range(K):
                    pe.wait_ge(s_diag, at(g, 2 * K, s + 1))
                    for n in range(N1):
                        u = s * N1 + n
                        if u < NB1:
                            pe.wait_ge(s_add, g * N2 + (u + 1))
                        else:
                            pe.wait_ge(s_ev, at(g, K * N1, u - NB1 + 1))
                        for k in range(NT):
                            last = nc.tensor.matmul(ps[u % NB1][:, 0:CH * W], diag[s % 2][:, k, :],
                                                    shifted(X[q], n * CH, n * CH + CH, k),
                                                    start=(k == 0), stop=(k == NT - 1))
                        last.then_inc(s_pe, 1)
                        if more and (s, n) == (2, 2):
                            pe.wait_ge(s_add, g * N2 + N2)
                            logits(g + 1)
                        if more and (s, n) == (2, N1 - 1):
                            spread(g + 1)
                if more:
                    pe.wait_ge(s_gate, gate_at(g + 1, "bc"))
                for s in range(K):
                    pe.wait_ge(s_diag, at(g, 2 * K, K + s + 1))
                    pe.wait_ge(s_ev, at(g, K * N1, K * N1))
                    for n in range(N2):
                        if n * CH + CH + 1 > R1 and (n - 1) * CH + CH + 1 <= R1:
                            pe.wait_ge(s_relu, at(g, K, s + 1))
                        for k in range(NT):
                            last = nc.tensor.matmul(ps[n][:, 0:CH * W], diag[(K + s) % 2][:, k, :],
                                                    shifted(Hd[s], n * CH, n * CH + CH, k),
                                                    start=(s == 0 and k == 0), stop=(s == K - 1 and k == NT - 1))
                        if s == K - 1:
                            last.then_inc(s_c2, 1)
                        elif n == N2 - 1:
                            last.then_inc(s_pe, 1)

            groups(pe, body)

        @block.vector
        def _(dve):
            dve.sem_inc(s_tap1, K * (NT - 1))
            dve.sem_inc(s_tap2, K * NT)
            dve.sem_inc(s_add, N2)
            dve.sem_inc(s_b2, B2_G)

            def stats(gi, li, q):
                dve.wait_ge(s_x[q], li * 32 + 32)
                base = gi * (NBN + 2)
                for n in range(NBN):
                    nc.vector.bn_stats(bn[:, n, :], inner(X[q], n * BN_ROWS, (n + 1) * BN_ROWS)).then_inc(s_bns, 1)
                nc.vector.tensor_reduce(c1(MX), inner(X[q], 0, H), axis=AX.XY, op=ALU.max).then_inc(s_bns, 1)
                dve.wait_ge(s_bns, base + NBN)
                nc.vector.tensor_copy(c1(14), m4[:, 0:1])
                nc.vector.bn_aggr(mv[:, :], bn[:, :, :].rearrange("p n s -> p (n s)")).then_inc(s_bns, 1)
                dve.wait_ge(s_bns, base + (NBN + 2))

            def step(gi, name, prev, ins):
                dve.wait_ge(s_gate, gate_at(gi, prev))
                ins().then_inc(s_gate, 1)

            def gate_norm(gi):
                nc.vector.tensor_scalar(c1(VEPS), mv[:, 1:2], GN_EPS, None, ALU.add).then_inc(s_gate, 1)
                nc.vector.tensor_scalar(c1(NEGM), mv[:, 0:1], -1.0, None, ALU.mult).then_inc(s_gate, 1)

            TS, TT, STT = nc.vector.tensor_scalar, nc.vector.tensor_tensor, nc.vector.scalar_tensor_tensor
            RED = nc.vector.tensor_reduce

            def gate_pool(gi):
                step(gi, "pool1", "center", lambda: STT(c1(P1), c1(MX), c1(NEGM), c1(RSTD), ALU.add, ALU.mult))
                step(gi, "pool2", "pool1", lambda: STT(c1(P2), c1(SUMC), 1.0 / PX, c1(RSTD), ALU.mult, ALU.mult))
                step(gi, "pooled", "pool2", lambda: TT(c1(PL), c1(P1), c1(P2), ALU.add))
                step(gi, "pmask", "pooled", lambda: TS(c1(PM, IMG), m4[:, :], c1(PL), None, ALU.mult))

            def gate_choose(gi):
                z0, z6 = z[:, 0:E], z[:, E:2 * E]
                gate, noise, minus = g_[:, 0:E], noi[:, 0:E], na[:, 0:E]
                gt, eq = sq6[:, 0], sq6[:, 1]
                other = lambda t: t.unsqueeze(1).broadcast_to([IMG, E, E])
                own = lambda t: t.unsqueeze(2).broadcast_to([IMG, E, E])
                hot = R[:, 0:K * E].rearrange("p (s e) -> p s e", s=K)
                gp3 = gp.rearrange("p (s e) -> p s e", s=K)
                step(gi, "z", "logits", lambda: TT(z[:, :], ps[7][0:IMG, 0:2 * E], fcb[:, :], ALU.add))
                step(gi, "g", "z", lambda: STT(gate, z0, 0.2, z0, ALU.mult, ALU.max))
                step(gi, "nabs", "z", lambda: STT(minus, z6, -1.0, z6, ALU.mult, ALU.min))
                step(gi, "noise", "ln", lambda: STT(noise, z6, 0.0, ln[:, 0:E], ALU.max, ALU.add))
                step(gi, "nsum", "noise", lambda: RED(nsum, noise, axis=AX.X, op=ALU.add))
                step(gi, "nmean", "nsum", lambda: TS(nmean, nsum, -1.0 / E, None, ALU.mult))
                step(gi, "dev", "nmean", lambda: TS(dev, noise, nmean, None, ALU.add))
                step(gi, "sq", "dev", lambda: TT(sq, dev, dev, ALU.mult))
                step(gi, "ss", "sq", lambda: RED(ss, sq, axis=AX.X, op=ALU.add))
                step(gi, "var", "ss", lambda: TS(var, ss, 1.0 / (E - 1), None, ALU.mult))
                step(gi, "score", "istd", lambda: STT(sc, dev, istd, gate, ALU.mult, ALU.add))
                step(gi, "gt", "score", lambda: TT(gt, other(sc), own(sc), ALU.is_gt))
                step(gi, "eq", "score", lambda: TT(eq, other(sc), own(sc), ALU.is_equal))
                step(gi, "tie", "eq", lambda: TT(eq, eq, tri[:, :, :], ALU.mult))
                step(gi, "cmp", "tie", lambda: TT(gt, gt, eq, ALU.add))
                step(gi, "rank", "cmp", lambda: RED(rank, gt, axis=AX.X, op=ALU.add))
                step(gi, "hot", "rank", lambda: TT(hot, rank.unsqueeze(1).broadcast_to([IMG, K, E]),
                                                   slots[:, :].unsqueeze(2).broadcast_to([IMG, K, E]), ALU.is_equal))
                step(gi, "gp", "hot", lambda: TT(gp3, hot, gate.unsqueeze(1).broadcast_to([IMG, K, E]), ALU.mult))
                step(gi, "gsel", "gp", lambda: RED(gsel, gp3, axis=AX.X, op=ALU.add))
                step(gi, "gmax", "gsel", lambda: RED(gmax, gsel, axis=AX.X, op=ALU.max))
                step(gi, "nmax", "gmax", lambda: TS(nmax, gmax, -1.0, None, ALU.mult))
                step(gi, "csum", "cexp", lambda: RED(csum, cexp, axis=AX.X, op=ALU.add))
                step(gi, "crec", "csum", lambda: nc.vector.reciprocal(crec, csum))
                step(gi, "cof", "crec", lambda: TS(R[:, K * E:K * E + K], cexp, crec, None, ALU.mult))

            def gate_weights(gi, q):
                step(gi, "bc", "bcast", lambda: nc.vector.tensor_copy(bc[:, :], ps[7][:, 0:K * E + K]))
                for s in range(K):
                    step(gi, f"pr{s}", "bc", lambda: TT(
                        prod[:, s], wall[:, :, :].rearrange("p e t -> p t e"),
                        bc[:, s * E:(s + 1) * E].unsqueeze(1).broadcast_to([P, 20, E]), ALU.mult))
                step(gi, "wsel", "pr2", lambda: RED(wsel[:, :, :].rearrange("p s t -> p (s t)"),
                                                    prod[:, :, :, :].rearrange("p s t e -> p (s t) e"),
                                                    axis=AX.X, op=ALU.add))
                cof = bc[:, K * E:K * E + K]
                step(gi, "w1", "wsel", lambda: TS(w1c[q][:, :, :], wsel[:, :, 0:9], c1(RSTD), None, ALU.mult))
                step(gi, "b1", "wsel", lambda: nc.vector.tensor_copy(b1c[q][:, :], wsel[:, :, 18]))
                step(gi, "w2", "wsel", lambda: TT(w2c[q][:, :, :], wsel[:, :, 9:18],
                                                  cof.unsqueeze(2).broadcast_to([P, K, NT]), ALU.mult))
                step(gi, "cb", "wsel", lambda: TT(cb[:, 0:K], wsel[:, :, 19], cof, ALU.mult))
                step(gi, "cbs", "cb", lambda: RED(cb[:, K:K + 1], cb[:, 0:K], axis=AX.X, op=ALU.add))
                step(gi, "bx", "cbs", lambda: TT(bxc[q][:, :], cb[:, K:K + 1], c1(NEGM), ALU.subtract))

            dve.wait_ge(s_const, 16 * NCONST)
            stats(0, 0, 0)
            gate_norm(0)
            gate_pool(0)
            gate_choose(0)
            gate_weights(0, 0)

            def body(g, i, q, more):
                for s in range(K):
                    for k in range(1, NT):
                        if k == 1:
                            dve.wait_ge(s_tap0, at(g, K, s + 1))
                        else:
                            dve.wait_ge(s_tap1, at(g, K * (NT - 1), s * (NT - 1) + k - 1))
                        STT(inner(Hd[s], R1, H), shifted(X[q], R1, H, k), w1c[q][:, s, k:k + 1],
                            inner(Hd[s], R1, H), ALU.mult, ALU.add).then_inc(s_tap1, 1)
                        if more and (s, k) == (1, NT - 1):
                            dve.wait_ge(s_gate, g * NG + NG)
                            stats(g + 1, i + q, 1 - q)
                            gate_norm(g + 1)
                        if more and (s, k) == (2, 3):
                            gate_pool(g + 1)
                        if more and (s, k) == (2, 5):
                            gate_choose(g + 1)
                if more:
                    gate_weights(g + 1, 1 - q)
                dve.wait_ge(s_xb, at(g, 1, 1))
                for s in range(K):
                    dve.wait_ge(s_relu, at(g, K, s + 1))
                    dve.wait_ge(s_ev, at(g, K * N1, (s + 1) * N1))
                    for k in range(NT):
                        if (s, k) != (0, 0):
                            dve.wait_ge(s_tap2, at(g, K * NT, s * NT + k))
                        STT(inner(X[q], R2, H), shifted(Hd[s], R2, H, k), w2c[q][:, s, k:k + 1],
                            inner(X[q], R2, H), ALU.mult, ALU.add).then_inc(s_tap2, 1)
                for n in range(N2):
                    dve.wait_ge(s_c2, at(g, N2, n + 1))
                    r = (n * CH, n * CH + CH)
                    STT(inner(X[q], *r), ps[n][:, 0:CH * W].rearrange("p (h w) -> p h w", h=CH), bxc[q][:, :],
                        inner(X[q], *r), ALU.add, ALU.add).then_inc(s_add, 1)
                dve.wait_ge(s_add, at(g, N2, N2))
                dve.wait_ge(s_tap2, at(g, K * NT, K * NT))
                dve.wait_ge(s_b2, g * B2_G + B2_G)
                for n in range(NBN):
                    nc.vector.bn_stats(bn1[:, n, :], inner(X[q], n * BN_ROWS, (n + 1) * BN_ROWS)).then_inc(s_b2, 1)
                dve.wait_ge(s_b2, at(g, B2_G, NBN))
                nc.vector.tensor_copy(c1(13), m4[:, 0:1])
                nc.vector.bn_aggr(mv1[:, :], bn1[:, :, :].rearrange("p n s -> p (n s)")).then_inc(s_b2, 1)
                dve.wait_ge(s_b2, at(g, B2_G, NBN + 1))
                TS(v1[:, 0:1], mv1[:, 1:2], GN_EPS, None, ALU.add).then_inc(s_b2, 1)
                dve.wait_ge(s_b2, at(g, B2_G, NBN + 3))
                dve.wait_ge(s_n2, g * 16 + 16)
                nc.vector.tensor_copy(st2[:, 0:1], v1[:, 1:2]).then_inc(s_b2, 1)
                STT(st2[:, 1:2], mv1[:, 0:1], -1.0, v1[:, 1:2], ALU.mult, ALU.mult).then_inc(s_b2, 1)

            groups(dve, body)

L_W, L_I, L_C, L_O = 1, 2, 3, 4
HALF = SPX // 2
HP3 = NPAIR // 2
UNITS = [(0, 1), (1, 1), (2, 1), (3, 1), (3, 0), (2, 0), (0, 0), (1, 0)]
PE_CONV = [(0, 0), (0, 4), (1, 0), (1, 4), (2, 0)]
DVE_CONV = [[(0, 1, 0, 8), (1, 1, 0, 8)], [(2, 1, 0, 8), (3, 1, 0, 8)], [(3, 0, 0, 8), (2, 0, 4, 4)]]
NPC = len(PE_CONV)
NTAP = sum(len(p) for p in DVE_CONV) * (NT - 1)
DVE_GELU = [u for p in DVE_CONV for u in p if u[1] == 0]
NW = 3


def filter_part(nc, x1, norm2, w_in, dw_k, filt, w_out, out):
    cas = hartley_pairs()
    cas_c = nc.inline_tensor(cas, name="hartley")
    back_c = nc.inline_tensor(np.ascontiguousarray(cas.T) / (T8 * T8), name="hartley_back")
    spread_c = nc.inline_tensor(filter_spread(), name="filter_spread")
    eye_c = nc.inline_tensor(np.eye(P, dtype=np.float32), name="eye2")
    og = out.rearrange("(g b) c h w -> g (b c) (h w)", b=IMG)
    x1a, n2a = x1.ap(), norm2.ap()

    with ExitStack() as ctx:
        def sb(name, shape):
            return ctx.enter_context(nc.sbuf_tensor(name, shape, F32))

        def sem(name):
            return ctx.enter_context(nc.semaphore(name))

        win = [sb(f"window{i}", [HID, IMG, 2, SR + 2, WP]) for i in range(NW)]
        Y = [sb(f"spectrum{i}", [P, NPAIR, IMG, H2]) for i in range(2)]
        g1 = [sb(f"gelu{i}", [HID, IMG, SPX]) for i in range(2)]
        y2 = sb("linear", [HID, IMG, SPX])
        xs = [sb(f"x1_strip{i}", [P, SPX]) for i in range(2)]
        xr = [sb(f"x1_again{i}", [P, SPX]) for i in range(2)]
        ob = [sb(f"out_strip{i}", [P, SPX]) for i in range(2)]
        xn = sb("normed", [P, NPAIR, P])
        xT = sb("pixels_first", [P, SPX])
        Xh = [sb(f"x_spectrum{i}", [P, SPX]) for i in range(2)]
        carrier = sb("carrier", [P, 2])
        nrm = sb("norm_scale_bias", [P, 2])
        cas_s, back, ident = sb("cas", [P, P]), sb("back", [P, P]), sb("ident2", [P, P])
        wbig = sb("w_in_by_image", [P, IMG, H2])
        filt_s = sb("filter", [P, H2])
        dg = sb("conv_diag", [HID, 2, NT, HID])
        dw = sb("conv_taps", [HID, 2, NT])
        wo = sb("w_out_t", [HID, C])
        spr = sb("spread", [T8 * NF, P])
        wn = sb("w_in_rows", [HID, 2, IMG, C])
        fn = sb("filter_rows", [HID, 2, T8 * NF])
        fT = sb("filter_t", [T8 * NF, H2])
        won = sb("w_out_rows", [C, HID])

        pX = ctx.enter_context(nc.psum_tensor("pX", [P, 512], F32))
        pC = ctx.enter_context(nc.psum_tensor("pC", [P, 512], F32))
        pW = ctx.enter_context(nc.psum_tensor("pW", [P, 2, 512], F32))
        pI = [ctx.enter_context(nc.psum_tensor(f"pI{i}", [P, 1024], F32)) for i in range(2)]

        s_c = sem("consts_loaded")
        s_sp = sem("setup_pe")
        s_sv = sem("setup_vector")
        s_z = sem("zeroed")
        s_nrm = sem("norm_loaded")
        s_xs = [sem(f"x1_loaded{i}") for i in range(2)]
        s_xr = [sem(f"x1_again_loaded{i}") for i in range(2)]
        s_os = [sem(f"out_stored{i}") for i in range(2)]
        s_xn = sem("x1_normed")
        s_T = sem("transposed")
        s_Te = sem("transposed_copied")
        s_D = sem("transformed")
        s_De = sem("transformed_copied")
        s_W = sem("w_in_done")
        s_We = sem("filtered")
        s_I = sem("pixels_back")
        s_Ie = sem("window_filled")
        s_cp = sem("pe_conv")
        s_gp = sem("pe_conv_gelu")
        s_t0 = sem("tap0")
        s_tp = sem("taps")
        s_gd = sem("vector_conv_gelu")
        s_m = sem("gated")
        s_O = sem("w_out_done")
        s_Oe = sem("residual_added")

        block = ctx.enter_context(nc.Block())
        N_UNIT, N_T0 = len(UNITS), 2 * len(DVE_CONV)
        NZ0 = NW + 2
        NC = 4 + IMG + 3
        PEEL = L_O + 2

        def need(eng, s, value):
            if not isinstance(value, int) or value > 0:
                eng.wait_ge(s, value)

        def nth(ks, kg):
            return kg * (NS // 2) + ks // 2

        def slots(eng, body):
            def slot(g, s, last):
                def strip(lag):
                    n = s - lag
                    if (isinstance(g, int) and g == 0 and not last and n < 0) or (last and n >= NS):
                        return None
                    return (g * NS + n, n % NS, g + n // NS)
                body(strip)
            for s in range(PEEL):
                slot(0, s, False)
            with eng.Fori(0, G - 1) as g:
                for s in range(PEEL, PEEL + NS):
                    slot(g, s, False)
            for s in range(PEEL, L_O + NS):
                slot(G - 1, s, True)

        def conv_ready(eng, k, ks, kg, j):
            if ks == NS - 1:
                need(eng, s_Ie, k * N_UNIT + j + 1)
                need(eng, s_z, kg * 2 + (NZ0 + 2))
            else:
                need(eng, s_Ie, k * N_UNIT + (N_UNIT + j + 1))

        def tap_rows(k_mod, b, h, r0, n, tap):
            dy, dx = TAPS[tap]
            return win[k_mod][:, b, h, r0 + dy:r0 + dy + n, dx:dx + W]

        def acc(ks, b, h, r0, n):
            t = g1[ks % 2] if h == 0 else y2
            return t[:, b, r0 * W:(r0 + n) * W].rearrange("p (r w) -> p r w", w=W)

        @block.sync
        def _(sp):
            cdma = lambda o, i: sp.dma_start(o, i).then_inc(s_c, 16)
            cdma(cas_s[:, :], cas_c.ap())
            cdma(back[:, :], back_c.ap())
            cdma(ident[:, :], eye_c.ap())
            cdma(spr[:, :], spread_c.ap())
            for b in range(IMG):
                cdma(wn[:, :, b, :], w_in.rearrange("(t h) c -> h t c", t=2))
            with nc.allow_non_contiguous_dma(reason="small weight tables, once"):
                cdma(fn[:, :, :], filt.rearrange("(t h) a e u v -> h t (a e u v)", t=2))
                cdma(dw[:, :, :], dw_k.rearrange("(t h) a u v -> h t (a u v)", t=2))
                cdma(won[:, :], w_out)

            def body(strip):
                if (st := strip(0)) is not None:
                    k, ks, kg = st
                    if ks == 0:
                        need(sp, s_xn, k)
                        sp.dma_start(nrm[:, :], n2a[kg]).then_inc(s_nrm, 16)
                    need(sp, s_xn, k - 1)
                    sp.dma_start(xs[ks % 2][:, :], x1a[kg][:, ks * SPX:(ks + 1) * SPX]).then_inc(s_xs[ks % 2], 16)
                if (st := strip(L_C)) is not None:
                    k, ks, kg = st
                    need(sp, s_Oe, (k - 1) * 2)
                    sp.dma_start(xr[ks % 2][:, :], x1a[kg][:, ks * SPX:(ks + 1) * SPX]).then_inc(s_xr[ks % 2], 16)
                if (st := strip(L_O)) is not None:
                    k, ks, kg = st
                    need(sp, s_Oe, k * 2 + 2)
                    sp.dma_start(og[kg][:, ks * SPX:(ks + 1) * SPX], ob[ks % 2][:, :]).then_inc(s_os[ks % 2], 16)

            slots(sp, body)
            for i in range(2):
                sp.wait_ge(s_os[i], G * NS // 2 * 16)

        @block.gpsimd
        def _(pool):
            for i in range(NW):
                nc.gpsimd.memset(win[i][:, :, :, :, :], 0.0).then_inc(s_z, 1)
            nc.gpsimd.memset(wbig[:, :, :], 0.0).then_inc(s_z, 1)
            nc.gpsimd.memset(carrier[:, :], 0.0).then_inc(s_z, 1)
            pool.wait_ge(s_z, NZ0)

            def zero(g):
                k = g * NS + (NS - 2)
                for s, n in ((s_cp, NPC), (s_tp, NTAP), (s_t0, N_T0)):
                    pool.wait_ge(s, k * n)
                pool.wait_ge(s_Ie, k * N_UNIT)
                nc.gpsimd.tensor_tensor(carrier[:, 1:2], carrier[:, 0:1], carrier[:, 0:1], ALU.add)
                nc.gpsimd.memset(win[(NS - 1) % NW][:, :, :, SR + 1, :], 0.0).then_inc(s_z, 1)
                nc.gpsimd.memset(win[0][:, :, :, 0, :], 0.0).then_inc(s_z, 1)

            with pool.Fori(0, G) as g:
                zero(g)

        @block.scalar
        def _(act):
            A = nc.scalar.activation

            def body(strip):
                sT, sI, sC = strip(0), strip(L_I), strip(L_C)
                if sT is not None:
                    k, ks, kg = sT
                    need(act, s_xs[ks % 2], nth(ks, kg) * 16 + 16)
                    if ks == 0:
                        need(act, s_nrm, kg * 16 + 16)
                    need(act, s_T, k * 2)
                    A(xn[:, :, :].rearrange("p q (r c) -> p q r c", r=SR),
                      xs[ks % 2][:, :].rearrange("p (r q c) -> p q r c", r=SR, q=NPAIR), ACT.Identity,
                      scale=nrm[:, 0:1], bias=nrm[:, 1:2]).then_inc(s_xn, 1)

                def fill(j):
                    if sI is None:
                        return
                    k, ks, kg = sI
                    b, h = UNITS[j]
                    need(act, s_I, k * N_UNIT + j + 1)
                    if j == 0:
                        need(act, s_cp, (k - 1) * NPC)
                        need(act, s_tp, (k - 1) * NTAP)
                        if isinstance(k, int) and k < NS:
                            need(act, s_z, NZ0)
                    p4 = pI[j % 2][0:HID, 0:SPX].rearrange("p (q r c) -> p q r c", q=NPAIR, r=SR)
                    row = lambda w, r: win[w][:, b, h, r, 1:1 + W].rearrange("p (q c) -> p q c", q=NPAIR)
                    if ks > 0:
                        A(row((ks - 1) % NW, SR + 1), p4[:, :, 0, :], ACT.Copy)
                    if ks < NS - 1:
                        A(row((ks + 1) % NW, 0), p4[:, :, SR - 1, :], ACT.Copy)
                    A(win[ks % NW][:, b, h, 1:SR + 1, 1:1 + W].rearrange("p r (q c) -> p q r c", q=NPAIR),
                      p4, ACT.Copy).then_inc(s_Ie, 1)

                def tap0(p):
                    if sC is None:
                        return
                    k, ks, kg = sC
                    for m, (b, h, r0, n) in enumerate(DVE_CONV[p]):
                        conv_ready(act, k, ks, kg, UNITS.index((b, h)))
                        if h:
                            need(act, s_m, k * IMG)
                        else:
                            need(act, s_O, (k - 1) * 2)
                        A(acc(ks, b, h, r0, n), tap_rows(ks % NW, b, h, r0, n, 0), ACT.Copy,
                          scale=dw[:, h, 0:1]).then_inc(s_t0, 1)

                def copy(sem_in, sem_out, dst, c):
                    k = sT[0]
                    need(act, sem_in, k * 2 + c + 1)
                    A(dst[:, c * HALF:(c + 1) * HALF], pX[:, 0:HALF], ACT.Copy).then_inc(sem_out, 1)

                def gelu_pe(c):
                    if sC is None:
                        return
                    k, ks, kg = sC
                    b, r0 = PE_CONV[c]
                    need(act, s_cp, k * NPC + c + 1)
                    if c == 0:
                        need(act, s_O, (k - 1) * 2)
                    A(g1[ks % 2][:, b, r0 * W:(r0 + 4) * W], pC[0:HID, 0:HALF], ACT.Gelu).then_inc(s_gp, 1)

                fill(0), fill(1), tap0(0), fill(2), fill(3), tap0(1), fill(4), fill(5), tap0(2)
                if sT is not None:
                    need(act, s_D, sT[0] * 2)
                    copy(s_T, s_Te, xT, 0)
                fill(6)
                if sT is not None:
                    copy(s_T, s_Te, xT, 1)
                fill(7)
                gelu_pe(0)
                if sT is not None:
                    need(act, s_W, (sT[0] - 1) * NPAIR)
                    copy(s_D, s_De, Xh[sT[1] % 2], 0)
                gelu_pe(1)
                if sT is not None:
                    copy(s_D, s_De, Xh[sT[1] % 2], 1)
                for c in range(2, NPC):
                    gelu_pe(c)
                if sC is not None:
                    k, ks, kg = sC
                    need(act, s_tp, k * NTAP + NTAP)
                    for b, h, r0, n in DVE_GELU:
                        t = acc(ks, b, h, r0, n)
                        A(t, t, ACT.Gelu).then_inc(s_gd, 1)

            slots(act, body)

        @block.tensor
        def _(pe):
            MM = nc.tensor.matmul
            pe.wait_ge(s_c, 16 * NC)
            for h in range(2):
                nc.tensor.transpose(pW[:, h, 0:HID], wn[:, h].rearrange("p b c -> p (b c)"), ident[0:HID, 0:HID])
            for h in range(2):
                nc.tensor.transpose(pI[0][0:T8 * NF, h * HID:(h + 1) * HID], fn[:, h, :], ident[0:HID, 0:HID])
            nc.tensor.transpose(pC[0:HID, 0:C], won[:, :], ident[0:C, 0:C]).then_inc(s_sp, 1)
            pe.wait_ge(s_sv, 1)
            MM(pI[1][:, 0:H2], spr[:, :], fT[:, :], start=True, stop=True).then_inc(s_sp, 1)
            pe.wait_ge(s_sv, 2)

            def body(strip):
                sT, sW, sI, sC, sO = (strip(n) for n in (0, L_W, L_I, L_C, L_O))

                def back_to_pixels(j):
                    if sI is None:
                        return
                    k, ks, kg = sI
                    b, h = UNITS[j]
                    if j == 0:
                        need(pe, s_We, k * NPAIR + NPAIR)
                    need(pe, s_Ie, k * N_UNIT + (j - 1))
                    for q in range(NPAIR):
                        last = MM(pI[j % 2][0:HID, q * P:(q + 1) * P], Y[ks % 2][:, q, b, h * HID:(h + 1) * HID],
                                  back[:, :], start=True, stop=True)
                    last.then_inc(s_I, 1)

                def w_in_pair(q):
                    if sW is None:
                        return
                    k, ks, kg = sW
                    if q == 0:
                        need(pe, s_De, k * 2 + 2)
                    need(pe, s_We, k * NPAIR + q)
                    for i in range(2):
                        last = MM(pW[:, i, 0:2 * H2], Xh[ks % 2][:, q * P:(q + 1) * P],
                                  wbig[:, 2 * i:2 * i + 2, :].rearrange("p b h -> p (b h)"), start=True, stop=True)
                    last.then_inc(s_W, 1)

                def transposes(c):
                    if sT is None:
                        return
                    k, ks, kg = sT
                    if c == 0:
                        need(pe, s_xn, k + 1)
                        need(pe, s_Oe, (k - L_O) * 2)
                        need(pe, s_De, k * 2)
                    else:
                        need(pe, s_Te, k * 2 + 1)
                    for j in range(HP3):
                        q = c * HP3 + j
                        last = nc.tensor.transpose(pX[:, j * P:(j + 1) * P], xn[:, q, :], ident[:, :])
                    last.then_inc(s_T, 1)

                def transform(c):
                    if sT is None:
                        return
                    k, ks, kg = sT
                    if c == 0:
                        need(pe, s_Te, k * 2 + 2)
                    else:
                        need(pe, s_De, k * 2 + 1)
                    for j in range(HP3):
                        q = c * HP3 + j
                        last = MM(pX[:, j * P:(j + 1) * P], xT[:, q * P:(q + 1) * P], cas_s[:, :], start=True, stop=True)
                    last.then_inc(s_D, 1)

                def conv(c):
                    if sC is None:
                        return
                    k, ks, kg = sC
                    b, r0 = PE_CONV[c]
                    conv_ready(pe, k, ks, kg, UNITS.index((b, 0)))
                    need(pe, s_gp, k * NPC + c)
                    for tap in range(NT):
                        last = MM(pC[0:HID, 0:HALF], dg[:, 0, tap, :], tap_rows(ks % NW, b, 0, r0, 4, tap),
                                  start=(tap == 0), stop=(tap == NT - 1))
                    last.then_inc(s_cp, 1)

                def w_out_half(c):
                    if sO is None:
                        return
                    k, ks, kg = sO
                    need(pe, s_m, k * IMG + IMG)
                    if c == 0:
                        if sT is not None:
                            need(pe, s_De, sT[0] * 2 + 2)
                        else:
                            need(pe, s_Oe, k * 2)
                    else:
                        need(pe, s_Oe, k * 2 + 1)
                    for b in range(IMG):
                        last = MM(pX[C * b:C * b + C, 0:HALF], wo[:, :], g1[ks % 2][:, b, c * HALF:(c + 1) * HALF],
                                  start=True, stop=True)
                    last.then_inc(s_O, 1)

                for j in range(NPAIR):
                    back_to_pixels(j)
                    w_in_pair(j)
                transposes(0), back_to_pixels(6), transposes(1), back_to_pixels(7)
                conv(0), transform(0), conv(1), transform(1), conv(2), w_out_half(0), conv(3), w_out_half(1)
                conv(4)

            slots(pe, body)

        @block.vector
        def _(dve):
            TT, STT = nc.vector.tensor_tensor, nc.vector.scalar_tensor_tensor
            dve.wait_ge(s_c, 16 * NC)
            for h in range(2):
                TT(dg[:, h], ident[0:HID, 0:HID].unsqueeze(1).broadcast_to([HID, NT, HID]),
                   dw[:, h, :].unsqueeze(2).broadcast_to([HID, NT, HID]), ALU.mult)
            dve.wait_ge(s_sp, 1)
            nc.vector.tensor_copy(fT[:, :], pI[0][0:T8 * NF, 0:H2]).then_inc(s_sv, 1)
            nc.vector.tensor_copy(wo[:, :], pC[0:HID, 0:C])
            dve.wait_ge(s_z, NZ0)
            for b in range(IMG):
                r = slice(C * b, C * b + C)
                nc.vector.tensor_copy(wbig[r, b, :].rearrange("p (t h) -> p t h", t=2), pW[r, :, 0:HID])
            dve.wait_ge(s_sp, 2)
            nc.vector.tensor_copy(filt_s[:, :], pI[1][:, 0:H2]).then_inc(s_sv, 1)
            dve.wait_ge(s_sv, 2)

            def body(strip):
                sW, sC, sO = strip(L_W), strip(L_C), strip(L_O)
                if sO is not None:
                    k, ks, kg = sO
                    need(dve, s_gp, k * NPC + NPC)
                    need(dve, s_gd, k * 2 + 2)
                    need(dve, s_tp, k * NTAP + NTAP)
                    for b in range(IMG):
                        t = g1[ks % 2][:, b, :]
                        TT(t, t, y2[:, b, :], ALU.mult).then_inc(s_m, 1)

                def filtered(q):
                    if sW is None:
                        return
                    k, ks, kg = sW
                    need(dve, s_W, k * NPAIR + q + 1)
                    if q == 0:
                        need(dve, s_I, (k - 1) * N_UNIT)
                    TT(Y[ks % 2][:, q].rearrange("p (i b) h -> p i b h", i=2),
                       pW[:, :, 0:2 * H2].rearrange("p i (b h) -> p i b h", b=2),
                       filt_s[:, :].unsqueeze(1).unsqueeze(1).broadcast_to([P, 2, 2, H2]), ALU.mult).then_inc(s_We, 1)

                def taps(a, z):
                    if sC is None:
                        return
                    k, ks, kg = sC
                    for n in range(a, z):
                        p, r = divmod(n, 2 * (NT - 1))
                        tap, m = r // 2 + 1, r % 2
                        b, h, r0, rows = DVE_CONV[p][m]
                        if tap == 1:
                            need(dve, s_t0, k * N_T0 + 2 * p + m + 1)
                        else:
                            need(dve, s_tp, k * NTAP + n - 1)
                        STT(acc(ks, b, h, r0, rows), tap_rows(ks % NW, b, h, r0, rows, tap), dw[:, h, tap:tap + 1],
                            acc(ks, b, h, r0, rows), ALU.mult, ALU.add).then_inc(s_tp, 1)

                def residual(c):
                    if sO is None:
                        return
                    k, ks, kg = sO
                    need(dve, s_O, k * 2 + c + 1)
                    if c == 0:
                        need(dve, s_xr[ks % 2], nth(ks, kg) * 16 + 16)
                        need(dve, s_os[ks % 2], nth(ks, kg) * 16)
                    r = slice(c * HALF, (c + 1) * HALF)
                    TT(ob[ks % 2][:, r], pX[:, 0:HALF], xr[ks % 2][:, r], ALU.add).then_inc(s_Oe, 1)

                filtered(0), filtered(1), taps(0, 2), filtered(2), taps(2, 5), filtered(3)
                taps(5, 8), filtered(4), taps(8, 11), filtered(5), taps(11, 40)
                residual(0), taps(40, NTAP), residual(1)

            slots(dve, body)


_INS = ["x", "L0_conv_fc0_w", "L0_conv_fc0_b", "L0_conv_fc1_w", "L0_conv_fc1_b", "L0_conv_w1", "L0_conv_b1",
        "L0_conv_w2", "L0_conv_b2", "L1_conv_w_in", "L1_conv_dw_k", "L1_conv_fft_filter", "L1_conv_w_out"]


def build(nc, x, fc0_w, fc0_b, fc1_w, fc1_b, w1, b1, w2, b2, w_in, dw_k, filt, w_out, out):
    x1 = nc.dram_tensor("x1", [G, P, PX], F32, kind="Internal")
    norm2 = nc.dram_tensor("norm2", [G, P, 2], F32, kind="Internal")
    experts_part(nc, x, fc0_w, fc0_b, fc1_w, fc1_b, w1, b1, w2, b2, x1, norm2)
    filter_part(nc, x1, norm2, w_in, dw_k, filt, w_out, out)


def kernel(**inputs):
    import numpy as _np
    import concourse.bacc as _bacc
    from concourse import mybir as _mybir
    from concourse.bass_utils import run_bass_kernel_spmd as _run

    nc = _bacc.Bacc("TRN2", target_bir_lowering=False, num_devices=1)
    arrays, args = {}, []
    for name in _INS:
        a = _np.ascontiguousarray(inputs[name])
        arrays[f"in_{name}_dram"] = a
        args.append(nc.dram_tensor(f"in_{name}_dram", a.shape, _mybir.dt.from_np(a.dtype), kind="ExternalInput").ap())
    out = nc.dram_tensor("out_0_dram", (B, C, H, W), F32, kind="ExternalOutput").ap()
    build(nc, *args, out)
    r = _run(nc, [arrays], core_ids=[0])
    return r.results[0]["out_0_dram"]
```

```python
from contextlib import ExitStack

import numpy as np

import concourse.bass as bass
from concourse import mybir

F32 = mybir.dt.float32
ALU = mybir.AluOpType
ACT = mybir.ActivationFunctionType
AX = mybir.AxisListType

P = 128
B, C, H, W = 32, 32, 96, 96
E, K = 6, 3
IMG = P // C
G = B // IMG
PX = H * W
WP = W + 2
HP = H + 2
TAPS = [(dy, dx) for dy in range(3) for dx in range(3)]
NT = len(TAPS)
GN_EPS = 1e-5

HID = 85
H2 = 2 * HID
T8 = 8
SR = T8
NS = H // SR
NPAIR = W // (2 * T8)
SPX = SR * W
NF = T8 // 2 + 1


def hartley_pairs():
    m = np.arange(T8)
    a = 2 * np.pi * ((m[:, None, None, None] * m[None, None, :, None]
                      + m[None, :, None, None] * m[None, None, None, :]) % T8) / T8
    cas = np.cos(a) + np.sin(a)
    full = np.zeros((T8, 2, T8, 2, T8, T8))
    for j in range(2):
        full[:, j, :, j] = cas
    return full.reshape(P, P).astype(np.float32)


def shift_angles():
    m = np.arange(T8)
    turn = np.array([[[((dy - 1) * u + (dx - 1) * v) % T8 for v in m] for u in m] for dy, dx in TAPS])
    a = 2 * np.pi * turn.reshape(NT, 1, T8 * T8) / T8
    return np.tile(np.concatenate([np.cos(a), np.sin(a)], 1), (1, 1, 2)).astype(np.float32)


def hartley_mirror(cas):
    m = (-np.arange(T8)) % T8
    return cas.reshape(P, 2, T8, T8)[:, :, m][:, :, :, m].reshape(P, P)


def border_columns():
    p = np.arange(P).reshape(T8, 2, T8)
    return np.concatenate([p[0].ravel(), p[-1].ravel(), p[:, :, 0].T.ravel(), p[:, :, -1].T.ravel()])


def filter_spread():
    s = np.zeros((T8, NF, 2, T8, T8))
    for u in range(T8):
        for v in range(T8):
            mu = (-u) % T8
            if v in (0, T8 // 2):
                s[u, v, :, u, v] += 0.5
                s[mu, v, :, u, v] += 0.5
            elif v < T8 // 2:
                s[u, v, :, u, v] = 1.0
            else:
                s[mu, T8 - v, :, u, v] = 1.0
    return s.reshape(T8 * NF, P).astype(np.float32)


CH = 5
R1, R2 = 40, 40
N1, N2 = R1 // CH, R2 // CH
NB1 = 6
BN_ROWS = 4
NBN = H // BN_ROWS

GATE = ["veps", "negm", "rstd", "center", "pool1", "pool2", "pooled", "pmask", "logits", "z", "g", "nabs",
        "exp", "ln", "noise", "nsum", "nmean", "dev", "sq", "ss", "var", "istd", "score", "gt", "eq", "tie",
        "cmp", "rank", "hot", "gp", "gsel", "gmax", "nmax", "cexp", "csum", "crec", "cof", "bcast", "bc",
        "pr0", "pr1", "pr2", "wsel", "w1", "b1", "w2", "cb", "cbs", "bx"]
NG = len(GATE)


def experts_part(nc, x, fc0_w, fc0_b, fc1_w, fc1_b, w1, b1, w2, b2, x1, norm2):
    mask = nc.inline_tensor(np.kron(np.eye(IMG), np.ones((C, 1))).astype(np.float32), name="image_mask")
    mask_t = nc.inline_tensor(np.kron(np.eye(IMG), np.ones((1, C))).astype(np.float32), name="image_mask_t")
    tri_c = nc.inline_tensor(np.tile(np.tril(np.ones((E, E)), -1).reshape(1, E, E), (IMG, 1, 1)).astype(np.float32), name="lower_first")
    slot_c = nc.inline_tensor(np.tile(np.arange(K).reshape(1, K), (IMG, 1)).astype(np.float32), name="slot_numbers")
    eye_c = nc.inline_tensor(np.eye(P, dtype=np.float32), name="eye1")

    xg = x.rearrange("(g b) c h w -> g (b c) h w", b=IMG)
    x1g = x1.ap().rearrange("g p (h w) -> g p h w", h=H)

    with ExitStack() as ctx:
        def sb(name, shape):
            return ctx.enter_context(nc.sbuf_tensor(name, shape, F32))

        def sem(name):
            return ctx.enter_context(nc.semaphore(name))

        X = [sb(f"x_pad{q}", [P, HP, WP]) for q in range(2)]
        Hd = [sb(f"hidden{s}", [P, HP, WP]) for s in range(K)]
        diag = [sb(f"diag{q}", [P, NT, P]) for q in range(2)]
        ident = sb("ident", [P, P])
        wall = sb("wall", [P, E, 20])
        fc = sb("fc", [P, 2 * E])
        fcb = sb("fcb", [IMG, 2 * E])
        m4 = sb("m4", [P, IMG])
        m4t = sb("m4t", [IMG, P])
        tri = sb("tri", [IMG, E, E])
        slots = sb("slots", [IMG, K])
        mhalf = sb("mhalf", [P, 1])
        bn = sb("bn", [P, NBN, 6])
        bn1 = sb("bn1", [P, NBN, 6])
        mv = sb("mv", [P, 2])
        mv1 = sb("mv1", [P, 2])
        col = sb("col", [P, 16])
        v1 = sb("v1", [P, 2])
        st2 = sb("st2", [P, 2])
        row = sb("row", [IMG, 160])
        sq6 = sb("sq6", [IMG, 2, E, E])
        R = sb("R", [IMG, K * E + K])
        bc = sb("bc", [P, K * E + K])
        prod = sb("prod", [P, K, 20, E])
        wsel = sb("wsel", [P, K, 20])
        w1c = [sb(f"w1c{q}", [P, K, NT]) for q in range(2)]
        w2c = [sb(f"w2c{q}", [P, K, NT]) for q in range(2)]
        b1c = [sb(f"b1c{q}", [P, K]) for q in range(2)]
        cb = sb("cb", [P, K + 1])
        bxc = [sb(f"bxc{q}", [P, 1]) for q in range(2)]
        ps = [ctx.enter_context(nc.psum_tensor(f"ps{i}", [P, 512], F32)) for i in range(8)]

        VEPS, NEGM, RSTD, MX, SUMC, P1, P2, PL, PM = 0, 1, 2, 3, 4, 5, 6, 7, 8
        c1 = lambda i, n=1: col[:, i:i + n]
        z, g_, na, ex, ln, noi = (row[:, 12 * i:12 * i + 12] for i in range(6))
        dev, sq, sc, rank = (row[:, 72 + 6 * i:78 + 6 * i] for i in range(4))
        nsum, nmean, ss, var, istd, gmax, nmax, csum, crec = (row[:, 96 + i:97 + i] for i in range(9))
        gsel, cexp = row[:, 106:109], row[:, 110:113]
        gp = row[:, 120:138]

        PE_G = K * N1 + K - 1
        B2_G = NBN + 5
        s_const = sem("const_loaded")
        s_set = sem("buffers_set")
        s_x = [sem(f"x_loaded{q}") for q in range(2)]
        s_st = [sem(f"x1_stored{q}") for q in range(2)]
        s_n2 = sem("norm2_stored")
        s_bns = sem("x_stats")
        s_gate = sem("gate_steps")
        s_pl = sem("gate_logits")
        s_diag = sem("diag_built")
        s_pe = sem("pe_units")
        s_c2 = sem("c2_pe_chunks")
        s_ev = sem("c1_pe_evacuated")
        s_tap0 = sem("c1_tap0")
        s_tap1 = sem("c1_taps")
        s_relu = sem("c1_relu")
        s_xb = sem("x_biased")
        s_tap2 = sem("c2_taps")
        s_add = sem("c2_pe_added")
        s_b2 = sem("x1_stats")

        block = ctx.enter_context(nc.Block())
        inner = lambda t, r0, r1: t[:, 1 + r0:1 + r1, 1:1 + W]
        shifted = lambda t, r0, r1, k: t[:, r0 + TAPS[k][0]:r1 + TAPS[k][0], TAPS[k][1]:TAPS[k][1] + W]
        gate_at = lambda g, name: g * NG + GATE.index(name) + 1
        at = lambda g, per, n: g * per + (per + n)
        NCONST = 5 + 7 * IMG + IMG

        def groups(eng, body):
            with eng.Fori(0, G // 2 - 1) as i:
                for q in range(2):
                    body(i * 2 + q, i, q, True)
            for q in range(2):
                body(G - 2 + q, G // 2 - 1, q, q == 0)

        @block.sync
        def _(sp):
            cdma = lambda o, i: sp.dma_start(o, i).then_inc(s_const, 16)
            for q in range(2):
                sp.sem_inc(s_st[q], 16)
            sp.sem_inc(s_n2, 16)
            sp.wait_ge(s_set, 1)
            for h in range(2):
                sp.dma_start(inner(X[0], 48 * h, 48 * h + 48), xg[0][:, 48 * h:48 * h + 48]).then_inc(s_x[0], 16)
            cdma(m4[:, :], mask.ap())
            cdma(m4t[:, :], mask_t.ap())
            cdma(tri[:, :, :], tri_c.ap())
            cdma(slots[:, :], slot_c.ap())
            cdma(ident[:, :], eye_c.ap())
            with nc.allow_non_contiguous_dma(reason="small weight tables, once"):
                for b in range(IMG):
                    o = slice(C * b, C * b + C)
                    cdma(fc[o, 0:E], fc1_w.rearrange("e c -> c e"))
                    cdma(fc[o, E:2 * E], fc0_w.rearrange("e c -> c e"))
                    cdma(wall[o, :, 0:9], w1.rearrange("e c a h w -> c e (a h w)"))
                    cdma(wall[o, :, 9:18], w2.rearrange("e c a h w -> c e (a h w)"))
                    cdma(wall[o, :, 18], b1.rearrange("e c -> c e"))
                    cdma(wall[o, :, 19], b2.rearrange("e c -> c e"))
                    cdma(fcb[b:b + 1, 0:E], fc1_b.rearrange("(a e) -> a e", a=1))
                    cdma(fcb[b:b + 1, E:2 * E], fc0_b.rearrange("(a e) -> a e", a=1))

            def body(g, i, q, more):
                if more:
                    sp.wait_ge(s_set, 2)
                    sp.wait_ge(s_st[1 - q], i * 16 + (16 + 16 * q))
                    for h in range(2):
                        sp.dma_start(inner(X[1 - q], 48 * h, 48 * h + 48),
                                     xg[g + 1][:, 48 * h:48 * h + 48]).then_inc(s_x[1 - q], 16)
                sp.wait_ge(s_add, at(g, N2, N2))
                sp.wait_ge(s_tap2, at(g, K * NT, K * NT))
                sp.dma_start(x1g[g], inner(X[q], 0, H)).then_inc(s_st[q], 16)
                sp.wait_ge(s_b2, at(g, B2_G, B2_G))
                sp.dma_start(norm2.ap()[g], st2[:, :]).then_inc(s_n2, 16)

            groups(sp, body)
            for q in range(2):
                sp.wait_ge(s_st[q], (G // 2 + 1) * 16)
            sp.wait_ge(s_n2, (G + 1) * 16)

        @block.gpsimd
        def _(pool):
            pool.sem_inc(s_diag, 2 * K)
            nc.gpsimd.memset(X[0][:, :, :], 0.0).then_inc(s_set, 1)
            nc.gpsimd.memset(X[1][:, :, :], 0.0).then_inc(s_set, 1)
            nc.gpsimd.memset(mhalf[:, :], -0.5).then_inc(s_set, 1)
            for s in range(K):
                nc.gpsimd.memset(Hd[s][:, :, :], 0.0).then_inc(s_set, 1)
            pool.wait_ge(s_const, 16 * NCONST)
            pool.wait_ge(s_set, 3)

            def rstd(gi):
                pool.wait_ge(s_gate, gate_at(gi, "negm"))
                nc.gpsimd.tensor_tensor(c1(RSTD), c1(VEPS), mhalf[:, :], ALU.pow).then_inc(s_gate, 1)

            def istd_(gi):
                pool.wait_ge(s_gate, gate_at(gi, "var"))
                nc.gpsimd.tensor_tensor(istd, var, mhalf[0:IMG, :], ALU.pow).then_inc(s_gate, 1)

            rstd(0)
            istd_(0)

            def body(g, i, q, more):
                for k in range(2 * K):
                    n = k - 2
                    if n == -2:
                        pool.wait_ge(s_gate, g * NG + NG)
                        pool.wait_ge(s_pe, g * PE_G + PE_G)
                    elif n == -1:
                        pool.wait_ge(s_c2, g * N2 + N2)
                    else:
                        pool.wait_ge(s_pe, at(g, PE_G, (n + 1) * N1 if n < K else K * N1 + n - K + 1))
                    wt = (w1c if k < K else w2c)[q][:, k % K, :]
                    nc.gpsimd.tensor_tensor(diag[k % 2][:, :, :],
                                            ident[:, :].unsqueeze(1).broadcast_to([P, NT, P]),
                                            wt.unsqueeze(2).broadcast_to([P, NT, P]), ALU.mult).then_inc(s_diag, 1)
                    if k == K and more:
                        rstd(g + 1)
                        istd_(g + 1)
                pool.wait_ge(s_b2, at(g, B2_G, NBN + 2))
                nc.gpsimd.tensor_tensor(v1[:, 1:2], v1[:, 0:1], mhalf[:, :], ALU.pow).then_inc(s_b2, 1)

            groups(pool, body)

        @block.scalar
        def _(act):
            act.sem_inc(s_ev, K * N1)
            act.sem_inc(s_tap0, K)
            act.sem_inc(s_relu, K)
            act.sem_inc(s_xb, 1)

            def center(gi, q):
                act.wait_ge(s_gate, gate_at(gi, "rstd"))
                act.wait_ge(s_bns, gi * (NBN + 2) + (NBN + 2))
                nc.scalar.activation(inner(X[q], 0, H), inner(X[q], 0, H), ACT.Identity,
                                     bias=c1(NEGM), accum_out=c1(SUMC)).then_inc(s_gate, 1)

            def gate_noise(gi):
                act.wait_ge(s_gate, gate_at(gi, "nabs"))
                nc.scalar.activation(ex[:, 0:E], na[:, 0:E], ACT.Exp).then_inc(s_gate, 1)
                act.wait_ge(s_gate, gate_at(gi, "exp"))
                nc.scalar.activation(ln[:, 0:E], ex[:, 0:E], ACT.Ln, bias=1.0).then_inc(s_gate, 1)

            def gate_softmax(gi):
                act.wait_ge(s_gate, gate_at(gi, "nmax"))
                nc.scalar.activation(cexp, gsel, ACT.Exp, bias=nmax).then_inc(s_gate, 1)

            act.wait_ge(s_set, 3 + K)
            center(0, 0)
            gate_noise(0)
            gate_softmax(0)

            def body(g, i, q, more):
                act.wait_ge(s_gate, g * NG + NG)
                for s in range(K):
                    act.wait_ge(s_tap2, g * (K * NT) + (s + 1) * NT)
                    if s < K - 1:
                        act.wait_ge(s_pe, g * PE_G + (K * N1 + s + 1))
                    else:
                        act.wait_ge(s_c2, g * N2 + N2)
                    nc.scalar.activation(inner(Hd[s], R1, H), shifted(X[q], R1, H, 0), ACT.Identity,
                                         scale=w1c[q][:, s, 0:1], bias=b1c[q][:, s:s + 1]).then_inc(s_tap0, 1)
                for s in range(K):
                    for n in range(N1):
                        u = s * N1 + n
                        act.wait_ge(s_pe, at(g, PE_G, u + 1))
                        nc.scalar.activation(inner(Hd[s], n * CH, n * CH + CH),
                                             ps[u % NB1][:, 0:CH * W].rearrange("p (h w) -> p h w", h=CH),
                                             ACT.Relu, bias=b1c[q][:, s:s + 1]).then_inc(s_ev, 1)
                        if more and (s, n) == (2, 1):
                            center(g + 1, 1 - q)
                        if more and (s, n) == (2, 4):
                            gate_noise(g + 1)
                            gate_softmax(g + 1)
                    act.wait_ge(s_tap1, at(g, K * (NT - 1), (s + 1) * (NT - 1)))
                    if s == K - 1:
                        nc.scalar.activation(inner(X[q], R2, H), inner(X[q], R2, H), ACT.Identity,
                                             bias=bxc[q][:, :]).then_inc(s_xb, 1)
                    nc.scalar.activation(inner(Hd[s], R1, H), inner(Hd[s], R1, H), ACT.Relu).then_inc(s_relu, 1)

            groups(act, body)

        @block.tensor
        def _(pe):
            pe.sem_inc(s_pe, PE_G)
            pe.sem_inc(s_c2, N2)

            def logits(gi):
                pe.wait_ge(s_gate, gate_at(gi, "pmask"))
                nc.tensor.matmul(ps[7][0:IMG, 0:2 * E], c1(PM, IMG), fc[:, :], start=True, stop=True).then_inc(s_gate, 1)

            def spread(gi):
                pe.wait_ge(s_gate, gate_at(gi, "cof"))
                nc.tensor.matmul(ps[7][:, 0:K * E + K], m4t[:, :], R[:, :], start=True, stop=True).then_inc(s_gate, 1)

            pe.wait_ge(s_const, 16 * NCONST)
            logits(0)
            spread(0)

            def body(g, i, q, more):
                for s in range(K):
                    pe.wait_ge(s_diag, at(g, 2 * K, s + 1))
                    for n in range(N1):
                        u = s * N1 + n
                        if u < NB1:
                            pe.wait_ge(s_add, g * N2 + (u + 1))
                        else:
                            pe.wait_ge(s_ev, at(g, K * N1, u - NB1 + 1))
                        for k in range(NT):
                            last = nc.tensor.matmul(ps[u % NB1][:, 0:CH * W], diag[s % 2][:, k, :],
                                                    shifted(X[q], n * CH, n * CH + CH, k),
                                                    start=(k == 0), stop=(k == NT - 1))
                        last.then_inc(s_pe, 1)
                        if more and (s, n) == (2, 2):
                            pe.wait_ge(s_add, g * N2 + N2)
                            logits(g + 1)
                        if more and (s, n) == (2, N1 - 1):
                            spread(g + 1)
                if more:
                    pe.wait_ge(s_gate, gate_at(g + 1, "bc"))
                for s in range(K):
                    pe.wait_ge(s_diag, at(g, 2 * K, K + s + 1))
                    pe.wait_ge(s_ev, at(g, K * N1, K * N1))
                    for n in range(N2):
                        if n * CH + CH + 1 > R1 and (n - 1) * CH + CH + 1 <= R1:
                            pe.wait_ge(s_relu, at(g, K, s + 1))
                        for k in range(NT):
                            last = nc.tensor.matmul(ps[n][:, 0:CH * W], diag[(K + s) % 2][:, k, :],
                                                    shifted(Hd[s], n * CH, n * CH + CH, k),
                                                    start=(s == 0 and k == 0), stop=(s == K - 1 and k == NT - 1))
                        if s == K - 1:
                            last.then_inc(s_c2, 1)
                        elif n == N2 - 1:
                            last.then_inc(s_pe, 1)

            groups(pe, body)

        @block.vector
        def _(dve):
            dve.sem_inc(s_tap1, K * (NT - 1))
            dve.sem_inc(s_tap2, K * NT)
            dve.sem_inc(s_add, N2)
            dve.sem_inc(s_b2, B2_G)

            def stats(gi, li, q):
                dve.wait_ge(s_x[q], li * 32 + 32)
                base = gi * (NBN + 2)
                for n in range(NBN):
                    nc.vector.bn_stats(bn[:, n, :], inner(X[q], n * BN_ROWS, (n + 1) * BN_ROWS)).then_inc(s_bns, 1)
                nc.vector.tensor_reduce(c1(MX), inner(X[q], 0, H), axis=AX.XY, op=ALU.max).then_inc(s_bns, 1)
                dve.wait_ge(s_bns, base + NBN)
                nc.vector.tensor_copy(c1(14), m4[:, 0:1])
                nc.vector.bn_aggr(mv[:, :], bn[:, :, :].rearrange("p n s -> p (n s)")).then_inc(s_bns, 1)
                dve.wait_ge(s_bns, base + (NBN + 2))

            def step(gi, name, prev, ins):
                dve.wait_ge(s_gate, gate_at(gi, prev))
                ins().then_inc(s_gate, 1)

            def gate_norm(gi):
                nc.vector.tensor_scalar(c1(VEPS), mv[:, 1:2], GN_EPS, None, ALU.add).then_inc(s_gate, 1)
                nc.vector.tensor_scalar(c1(NEGM), mv[:, 0:1], -1.0, None, ALU.mult).then_inc(s_gate, 1)

            TS, TT, STT = nc.vector.tensor_scalar, nc.vector.tensor_tensor, nc.vector.scalar_tensor_tensor
            RED = nc.vector.tensor_reduce

            def gate_pool(gi):
                step(gi, "pool1", "center", lambda: STT(c1(P1), c1(MX), c1(NEGM), c1(RSTD), ALU.add, ALU.mult))
                step(gi, "pool2", "pool1", lambda: STT(c1(P2), c1(SUMC), 1.0 / PX, c1(RSTD), ALU.mult, ALU.mult))
                step(gi, "pooled", "pool2", lambda: TT(c1(PL), c1(P1), c1(P2), ALU.add))
                step(gi, "pmask", "pooled", lambda: TS(c1(PM, IMG), m4[:, :], c1(PL), None, ALU.mult))

            def gate_choose(gi):
                z0, z6 = z[:, 0:E], z[:, E:2 * E]
                gate, noise, minus = g_[:, 0:E], noi[:, 0:E], na[:, 0:E]
                gt, eq = sq6[:, 0], sq6[:, 1]
                other = lambda t: t.unsqueeze(1).broadcast_to([IMG, E, E])
                own = lambda t: t.unsqueeze(2).broadcast_to([IMG, E, E])
                hot = R[:, 0:K * E].rearrange("p (s e) -> p s e", s=K)
                gp3 = gp.rearrange("p (s e) -> p s e", s=K)
                step(gi, "z", "logits", lambda: TT(z[:, :], ps[7][0:IMG, 0:2 * E], fcb[:, :], ALU.add))
                step(gi, "g", "z", lambda: STT(gate, z0, 0.2, z0, ALU.mult, ALU.max))
                step(gi, "nabs", "z", lambda: STT(minus, z6, -1.0, z6, ALU.mult, ALU.min))
                step(gi, "noise", "ln", lambda: STT(noise, z6, 0.0, ln[:, 0:E], ALU.max, ALU.add))
                step(gi, "nsum", "noise", lambda: RED(nsum, noise, axis=AX.X, op=ALU.add))
                step(gi, "nmean", "nsum", lambda: TS(nmean, nsum, -1.0 / E, None, ALU.mult))
                step(gi, "dev", "nmean", lambda: TS(dev, noise, nmean, None, ALU.add))
                step(gi, "sq", "dev", lambda: TT(sq, dev, dev, ALU.mult))
                step(gi, "ss", "sq", lambda: RED(ss, sq, axis=AX.X, op=ALU.add))
                step(gi, "var", "ss", lambda: TS(var, ss, 1.0 / (E - 1), None, ALU.mult))
                step(gi, "score", "istd", lambda: STT(sc, dev, istd, gate, ALU.mult, ALU.add))
                step(gi, "gt", "score", lambda: TT(gt, other(sc), own(sc), ALU.is_gt))
                step(gi, "eq", "score", lambda: TT(eq, other(sc), own(sc), ALU.is_equal))
                step(gi, "tie", "eq", lambda: TT(eq, eq, tri[:, :, :], ALU.mult))
                step(gi, "cmp", "tie", lambda: TT(gt, gt, eq, ALU.add))
                step(gi, "rank", "cmp", lambda: RED(rank, gt, axis=AX.X, op=ALU.add))
                step(gi, "hot", "rank", lambda: TT(hot, rank.unsqueeze(1).broadcast_to([IMG, K, E]),
                                                   slots[:, :].unsqueeze(2).broadcast_to([IMG, K, E]), ALU.is_equal))
                step(gi, "gp", "hot", lambda: TT(gp3, hot, gate.unsqueeze(1).broadcast_to([IMG, K, E]), ALU.mult))
                step(gi, "gsel", "gp", lambda: RED(gsel, gp3, axis=AX.X, op=ALU.add))
                step(gi, "gmax", "gsel", lambda: RED(gmax, gsel, axis=AX.X, op=ALU.max))
                step(gi, "nmax", "gmax", lambda: TS(nmax, gmax, -1.0, None, ALU.mult))
                step(gi, "csum", "cexp", lambda: RED(csum, cexp, axis=AX.X, op=ALU.add))
                step(gi, "crec", "csum", lambda: nc.vector.reciprocal(crec, csum))
                step(gi, "cof", "crec", lambda: TS(R[:, K * E:K * E + K], cexp, crec, None, ALU.mult))

            def gate_weights(gi, q):
                step(gi, "bc", "bcast", lambda: nc.vector.tensor_copy(bc[:, :], ps[7][:, 0:K * E + K]))
                for s in range(K):
                    step(gi, f"pr{s}", "bc", lambda: TT(
                        prod[:, s], wall[:, :, :].rearrange("p e t -> p t e"),
                        bc[:, s * E:(s + 1) * E].unsqueeze(1).broadcast_to([P, 20, E]), ALU.mult))
                step(gi, "wsel", "pr2", lambda: RED(wsel[:, :, :].rearrange("p s t -> p (s t)"),
                                                    prod[:, :, :, :].rearrange("p s t e -> p (s t) e"),
                                                    axis=AX.X, op=ALU.add))
                cof = bc[:, K * E:K * E + K]
                step(gi, "w1", "wsel", lambda: TS(w1c[q][:, :, :], wsel[:, :, 0:9], c1(RSTD), None, ALU.mult))
                step(gi, "b1", "wsel", lambda: nc.vector.tensor_copy(b1c[q][:, :], wsel[:, :, 18]))
                step(gi, "w2", "wsel", lambda: TT(w2c[q][:, :, :], wsel[:, :, 9:18],
                                                  cof.unsqueeze(2).broadcast_to([P, K, NT]), ALU.mult))
                step(gi, "cb", "wsel", lambda: TT(cb[:, 0:K], wsel[:, :, 19], cof, ALU.mult))
                step(gi, "cbs", "cb", lambda: RED(cb[:, K:K + 1], cb[:, 0:K], axis=AX.X, op=ALU.add))
                step(gi, "bx", "cbs", lambda: TT(bxc[q][:, :], cb[:, K:K + 1], c1(NEGM), ALU.subtract))

            dve.wait_ge(s_const, 16 * NCONST)
            stats(0, 0, 0)
            gate_norm(0)
            gate_pool(0)
            gate_choose(0)
            gate_weights(0, 0)

            def body(g, i, q, more):
                for s in range(K):
                    for k in range(1, NT):
                        if k == 1:
                            dve.wait_ge(s_tap0, at(g, K, s + 1))
                        else:
                            dve.wait_ge(s_tap1, at(g, K * (NT - 1), s * (NT - 1) + k - 1))
                        STT(inner(Hd[s], R1, H), shifted(X[q], R1, H, k), w1c[q][:, s, k:k + 1],
                            inner(Hd[s], R1, H), ALU.mult, ALU.add).then_inc(s_tap1, 1)
                        if more and (s, k) == (1, NT - 1):
                            dve.wait_ge(s_gate, g * NG + NG)
                            stats(g + 1, i + q, 1 - q)
                            gate_norm(g + 1)
                        if more and (s, k) == (2, 3):
                            gate_pool(g + 1)
                        if more and (s, k) == (2, 5):
                            gate_choose(g + 1)
                if more:
                    gate_weights(g + 1, 1 - q)
                dve.wait_ge(s_xb, at(g, 1, 1))
                for s in range(K):
                    dve.wait_ge(s_relu, at(g, K, s + 1))
                    dve.wait_ge(s_ev, at(g, K * N1, (s + 1) * N1))
                    for k in range(NT):
                        if (s, k) != (0, 0):
                            dve.wait_ge(s_tap2, at(g, K * NT, s * NT + k))
                        STT(inner(X[q], R2, H), shifted(Hd[s], R2, H, k), w2c[q][:, s, k:k + 1],
                            inner(X[q], R2, H), ALU.mult, ALU.add).then_inc(s_tap2, 1)
                for n in range(N2):
                    dve.wait_ge(s_c2, at(g, N2, n + 1))
                    r = (n * CH, n * CH + CH)
                    STT(inner(X[q], *r), ps[n][:, 0:CH * W].rearrange("p (h w) -> p h w", h=CH), bxc[q][:, :],
                        inner(X[q], *r), ALU.add, ALU.add).then_inc(s_add, 1)
                dve.wait_ge(s_add, at(g, N2, N2))
                dve.wait_ge(s_tap2, at(g, K * NT, K * NT))
                dve.wait_ge(s_b2, g * B2_G + B2_G)
                for n in range(NBN):
                    nc.vector.bn_stats(bn1[:, n, :], inner(X[q], n * BN_ROWS, (n + 1) * BN_ROWS)).then_inc(s_b2, 1)
                dve.wait_ge(s_b2, at(g, B2_G, NBN))
                nc.vector.tensor_copy(c1(13), m4[:, 0:1])
                nc.vector.bn_aggr(mv1[:, :], bn1[:, :, :].rearrange("p n s -> p (n s)")).then_inc(s_b2, 1)
                dve.wait_ge(s_b2, at(g, B2_G, NBN + 1))
                TS(v1[:, 0:1], mv1[:, 1:2], GN_EPS, None, ALU.add).then_inc(s_b2, 1)
                dve.wait_ge(s_b2, at(g, B2_G, NBN + 3))
                dve.wait_ge(s_n2, g * 16 + 16)
                nc.vector.tensor_copy(st2[:, 0:1], v1[:, 1:2]).then_inc(s_b2, 1)
                STT(st2[:, 1:2], mv1[:, 0:1], -1.0, v1[:, 1:2], ALU.mult, ALU.mult).then_inc(s_b2, 1)

            groups(dve, body)

L_W, L_I, L_C, L_O = 1, 2, 3, 4
HALF = SPX // 2
HP3 = NPAIR // 2
CA = P // 2
CB = HID - CA
HC = IMG * HID
TILE = [(0, P), (P, P), (2 * P, IMG * CB)]
LAST, MB = 2, IMG * CB
UNITS = [(1, 0), (1, 1), (1, 2), (0, 0), (0, 1), (0, 2)]
NU = len(UNITS)
NJ = W // T8
NBD = 4 * T8
BSTR = W + 2 * T8
BOFF = T8
BW = BOFF + 4 * BSTR
NTAB = 3
NZB = 3
NFIX = 24


def filter_part(nc, x1, norm2, w_in, dw_k, filt, w_out, out):
    cas = hartley_pairs()
    n64 = np.float32(T8 * T8)
    back_n = np.ascontiguousarray(cas.T) / n64
    cas_c = nc.inline_tensor(cas, name="hartley")
    back_c = nc.inline_tensor(back_n, name="hartley_back")
    mirror_c = nc.inline_tensor(np.ascontiguousarray(hartley_mirror(cas).T) / n64, name="hartley_back_mirror")
    border_c = nc.inline_tensor(np.ascontiguousarray(back_n[:, border_columns()]), name="hartley_back_border")
    angle_c = nc.inline_tensor(shift_angles(), name="shift_angles")
    spread_c = nc.inline_tensor(filter_spread(), name="filter_spread")
    eye_c = nc.inline_tensor(np.eye(P, dtype=np.float32), name="eye2")
    og = out.rearrange("(g b) c h w -> g (b c) (h w)", b=IMG)
    x1a, n2a = x1.ap(), norm2.ap()

    with ExitStack() as ctx:
        def sb(name, shape):
            return ctx.enter_context(nc.sbuf_tensor(name, shape, F32))

        def sem(name):
            return ctx.enter_context(nc.semaphore(name))

        xs = [sb(f"x1_strip{i}", [P, SPX]) for i in range(2)]
        xr = [sb(f"x1_again{i}", [P, SPX]) for i in range(2)]
        xn = sb("normed", [P, NPAIR, P])
        xT = sb("pixels_first", [P, SPX])
        Xh = [sb(f"x_spectrum{i}", [P, SPX]) for i in range(2)]
        Y = [sb(f"spectrum{i}", [P, NTAB, HP3, 2 * HC]) for i in range(3)]
        z = [sb(f"hidden_pixels{i}", [P, 2, 3, SPX]) for i in range(2)]
        bd = [sb(f"border{i}", [P, NU, BW]) for i in range(3)]
        dT = sb("step_top", [P, NU, NJ, T8 + 2])
        dB = sb("step_bottom", [P, NU, NJ, T8 + 2])
        dL = sb("step_left", [P, NU, T8, NJ])
        dR = sb("step_right", [P, NU, T8, NJ])
        nrm = sb("norm_scale_bias", [P, 2])
        cas_s, back, mirror, ident = (sb(n, [P, P]) for n in ("cas", "back", "back_mirror", "ident2"))
        border = sb("back_border", [P, 2 * NBD])
        wbig = sb("w_in_by_image", [P, 2, HC])
        ftab = sb("filters", [P, NTAB, 2, HC])
        dg = sb("conv_diag", [MB, 2, NT, MB])
        kt = sb("conv_taps", [P, 2, 2, NT])
        wo = sb("w_out_by_image", [P, 3, P])
        wn = sb("w_in_rows", [HID, 2, IMG, C])
        fn = sb("filter_rows", [HID, 2, T8 * NF])
        kn = sb("tap_rows", [HID, 2, NT])
        fT = sb("filter_t", [T8 * NF, H2])
        kT = sb("taps_t", [NT, H2])
        fs = sb("filters_once", [P, NTAB, H2])
        spr = sb("spread", [T8 * NF, P])
        ang = sb("angles", [NT, 2, P])
        won = sb("w_out_rows", [P, HC])

        pX = ctx.enter_context(nc.psum_tensor("pX", [P, 512], F32))
        pW = ctx.enter_context(nc.psum_tensor("pW", [P, 2, 512], F32))
        pV = ctx.enter_context(nc.psum_tensor("pV", [P, 2, 512], F32))
        pZ = [ctx.enter_context(nc.psum_tensor(f"pZ{i}", [P, 512], F32)) for i in range(NZB)]

        s_c = sem("consts_loaded")
        s_sp = sem("setup_pe")
        s_sv = sem("setup_vector")
        s_z = sem("zeroed")
        s_nrm = sem("norm_loaded")
        s_xs = [sem(f"x1_loaded{i}") for i in range(2)]
        s_xr = [sem(f"x1_again_loaded{i}") for i in range(2)]
        s_os = [sem(f"out_stored{i}") for i in range(2)]
        s_xn = sem("x1_normed")
        s_T = sem("transposed")
        s_Te = sem("transposed_copied")
        s_D = sem("transformed")
        s_De = sem("transformed_copied")
        s_W = sem("w_in_done")
        s_We = sem("filtered")
        s_B = sem("border_back")
        s_Be = sem("border_copied")
        s_I = sem("pixels_back")
        s_Ie = sem("pixels_copied")
        s_st = sem("steps_made")
        s_fx = sem("borders_fixed")
        s_cp = sem("third_tile_taps")
        s_ca = sem("third_tile_fixed")
        s_g = sem("gelu_done")
        s_m = sem("gated")
        s_O = sem("w_out_done")
        s_Oe = sem("residual_added")

        block = ctx.enter_context(nc.Block())
        NZ0 = 7
        NCD = 6 + IMG + 2 + 2 + IMG + 2 * IMG + 1
        PEEL = L_O + 2

        def need(eng, s, value):
            if not isinstance(value, int) or value > 0:
                eng.wait_ge(s, value)

        def nth(ks, kg):
            return kg * (NS // 2) + ks // 2

        def slots(eng, body):
            def slot(g, s, last):
                def strip(lag):
                    n = s - lag
                    if (isinstance(g, int) and g == 0 and not last and n < 0) or (last and n >= NS):
                        return None
                    return (g * NS + n, n % NS, g + n // NS)
                body(strip)
            for s in range(PEEL):
                slot(0, s, False)
            with eng.Fori(0, G - 1) as g:
                for s in range(PEEL, PEEL + NS):
                    slot(g, s, False)
            for s in range(PEEL, L_O + NS):
                slot(G - 1, s, True)

        def spectrum(ks, q):
            return Y[(2 * ks + q // HP3) % 3], q % HP3

        @block.sync
        def _(sp):
            cdma = lambda o, i: sp.dma_start(o, i).then_inc(s_c, 16)
            cdma(cas_s[:, :], cas_c.ap())
            cdma(back[:, :], back_c.ap())
            cdma(mirror[:, :], mirror_c.ap())
            cdma(border[:, :], border_c.ap())
            cdma(ident[:, :], eye_c.ap())
            cdma(spr[:, :], spread_c.ap())
            cdma(ang[:, :, :], angle_c.ap())
            with nc.allow_non_contiguous_dma(reason="small weight tables, once"):
                cdma(fn[:, :, :], filt.rearrange("(t h) a e u v -> h t (a e u v)", t=2))
                taps = dw_k.rearrange("(t h) a u v -> h t (a u v)", t=2)
                cdma(kn[:, :, :], taps)
                for b in range(2):
                    cdma(kt[b * CA:b * CA + CA, 0], taps[0:CA])
                for b in range(IMG):
                    cdma(kt[b * CB:b * CB + CB, 1], taps[CA:HID])
                for b in range(IMG):
                    cdma(wn[:, :, b, :], w_in.rearrange("(t h) c -> h t c", t=2))
                sp.wait_ge(s_z, 1)
                for b in range(IMG):
                    r = slice(b * C, b * C + C)
                    cdma(won[r, b * CA:b * CA + CA], w_out[:, 0:CA])
                    cdma(won[r, IMG * CA + b * CB:IMG * CA + b * CB + CB], w_out[:, CA:HID])

            def body(strip):
                if (st := strip(0)) is not None:
                    k, ks, kg = st
                    if ks == 0:
                        need(sp, s_xn, k)
                        sp.dma_start(nrm[:, :], n2a[kg]).then_inc(s_nrm, 16)
                    need(sp, s_xn, k - 1)
                    sp.dma_start(xs[ks % 2][:, :], x1a[kg][:, ks * SPX:(ks + 1) * SPX]).then_inc(s_xs[ks % 2], 16)
                if (st := strip(L_C)) is not None:
                    k, ks, kg = st
                    need(sp, s_os[ks % 2], nth(ks, kg) * 16)
                    sp.dma_start(xr[ks % 2][:, :], x1a[kg][:, ks * SPX:(ks + 1) * SPX]).then_inc(s_xr[ks % 2], 16)
                if (st := strip(L_O)) is not None:
                    k, ks, kg = st
                    need(sp, s_Oe, k * 2 + 2)
                    sp.dma_start(og[kg][:, ks * SPX:(ks + 1) * SPX], xr[ks % 2][:, :]).then_inc(s_os[ks % 2], 16)

            slots(sp, body)
            for i in range(2):
                sp.wait_ge(s_os[i], G * NS // 2 * 16)

        @block.gpsimd
        def _(pool):
            nc.gpsimd.memset(won[:, :], 0.0).then_inc(s_z, 1)
            nc.gpsimd.memset(wbig[:, :, :], 0.0).then_inc(s_z, 1)
            for i in range(3):
                nc.gpsimd.memset(bd[i][:, :, :], 0.0).then_inc(s_z, 1)
            for i in range(2):
                nc.gpsimd.memset(z[i][:, :, :, :], 0.0).then_inc(s_z, 1)

        @block.scalar
        def _(act):
            A = nc.scalar.activation
            act.wait_ge(s_z, NZ0)

            def body(strip):
                sT, sI, sC = strip(0), strip(L_I), strip(L_C)
                if sT is not None:
                    k, ks, kg = sT
                    need(act, s_xs[ks % 2], nth(ks, kg) * 16 + 16)
                    if ks == 0:
                        need(act, s_nrm, kg * 16 + 16)
                    need(act, s_T, k * 2)
                    A(xn[:, :, :].rearrange("p q (r c) -> p q r c", r=SR),
                      xs[ks % 2][:, :].rearrange("p (r q c) -> p q r c", r=SR, q=NPAIR), ACT.Identity,
                      scale=nrm[:, 0:1], bias=nrm[:, 1:2]).then_inc(s_xn, 1)

                def border_out(j):
                    if sI is None:
                        return
                    k, ks, kg = sI
                    h, i = UNITS[j]
                    m = TILE[i][1]
                    need(act, s_B, k * NU + j + 1)
                    if j == 0:
                        need(act, s_st, k - 1)
                    A(bd[ks % 3][0:m, j, BOFF:BOFF + 4 * BSTR].rearrange("p (s e) -> p s e", s=4)[:, :, 0:W]
                      .rearrange("p s (q c) -> p q s c", q=NPAIR),
                      pV[0:m, j % 2, 0:2 * NBD * NPAIR].rearrange("p (q s c) -> p q s c", q=NPAIR, s=4),
                      ACT.Copy).then_inc(s_Be, 1)

                def pixels_out(c, j):
                    if sI is None:
                        return
                    k, ks, kg = sI
                    h, i = UNITS[j]
                    n, m = c * NU + j, TILE[i][1]
                    need(act, s_I, k * (2 * NU) + n + 1)
                    if n == 0:
                        need(act, s_m, (k - 1) * 2)
                    if (c, h) == (0, 0):
                        need(act, s_O, (k - 1) * 2)
                    A(z[ks % 2][0:m, h, i, :].rearrange("p (r q c) -> p q r c", r=SR, q=NPAIR)[:, c * HP3:(c + 1) * HP3],
                      pZ[n % NZB][0:m, 0:HALF].rearrange("p (q r c) -> p q r c", q=HP3, r=SR),
                      ACT.Copy).then_inc(s_Ie, 1)

                def copy(sem_in, sem_out, dst, c):
                    if sT is None:
                        return
                    k = sT[0]
                    need(act, sem_in, k * 2 + c + 1)
                    A(dst[:, c * HALF:(c + 1) * HALF], pX[:, 0:HALF], ACT.Copy).then_inc(sem_out, 1)

                for j in range(NU):
                    border_out(j)
                for j in range(NU):
                    pixels_out(0, j)
                pixels_out(1, 0)
                if sT is not None:
                    need(act, s_D, sT[0] * 2)
                copy(s_T, s_Te, xT, 0)
                pixels_out(1, 1)
                pixels_out(1, 2)
                copy(s_T, s_Te, xT, 1)
                pixels_out(1, 3)
                pixels_out(1, 4)
                if sT is not None:
                    need(act, s_W, (sT[0] - 1) * NPAIR)
                copy(s_D, s_De, Xh[strip(0)[1] % 2] if sT is not None else None, 0)
                pixels_out(1, 5)
                copy(s_D, s_De, Xh[strip(0)[1] % 2] if sT is not None else None, 1)
                if sC is not None:
                    k, ks, kg = sC
                    need(act, s_ca, k * 2 + 2)
                    need(act, s_fx, k * NFIX + NFIX)
                    for c in range(2):
                        t = z[ks % 2][:, 0, :, c * HALF:(c + 1) * HALF]
                        A(t, t, ACT.Gelu).then_inc(s_g, 1)

            slots(act, body)

        @block.tensor
        def _(pe):
            MM = nc.tensor.matmul
            pe.wait_ge(s_c, 16 * NCD)
            for h in range(2):
                nc.tensor.transpose(pZ[0][:, h * HID:(h + 1) * HID], wn[:, h].rearrange("p b c -> p (b c)"), ident[0:HID, 0:HID])
                nc.tensor.transpose(pZ[1][0:T8 * NF, h * HID:(h + 1) * HID], fn[:, h, :], ident[0:HID, 0:HID])
                nc.tensor.transpose(pZ[2][0:NT, h * HID:(h + 1) * HID], kn[:, h, :], ident[0:HID, 0:HID])
            for i, (o, m) in enumerate(TILE):
                last = nc.tensor.transpose(pX[0:m, i * P:(i + 1) * P], won[:, o:o + m], ident[:, :])
            last.then_inc(s_sp, 1)
            pe.wait_ge(s_sv, 1)
            MM(pV[:, 0, 0:H2], spr[:, :], fT[:, :], start=True, stop=True)
            for i in range(2):
                last = MM(pW[:, i, 0:H2], ang[:, i, :], kT[:, :], start=True, stop=True)
            last.then_inc(s_sp, 1)
            pe.wait_ge(s_sv, 5)

            def body(strip):
                sT, sW, sI, sC, sO = (strip(n) for n in (0, L_W, L_I, L_C, L_O))

                def border_back(j):
                    if sI is None:
                        return
                    k, ks, kg = sI
                    h, i = UNITS[j]
                    o, m = TILE[i]
                    if j == 0:
                        need(pe, s_We, k * NPAIR + NPAIR)
                        need(pe, s_ca, (k - 1) * 2)
                    need(pe, s_Be, k * NU + (j - 1))
                    for q in range(NPAIR):
                        y, n = spectrum(ks, q)
                        last = MM(pV[0:m, j % 2, q * 2 * NBD:(q + 1) * 2 * NBD], y[:, 0, n, h * HC + o:h * HC + o + m],
                                  border[:, :], start=True, stop=True)
                    last.then_inc(s_B, 1)

                def pixels_back(c, j):
                    if sI is None:
                        return
                    k, ks, kg = sI
                    h, i = UNITS[j]
                    o, m = TILE[i]
                    u = c * NU + j
                    need(pe, s_Ie, k * (2 * NU) + (u - NZB + 1))
                    for q in range(c * HP3, (c + 1) * HP3):
                        y, n = spectrum(ks, q)
                        r = slice((q % HP3) * P, (q % HP3 + 1) * P)
                        MM(pZ[u % NZB][0:m, r], y[:, 1, n, h * HC + o:h * HC + o + m], back[:, :], start=True, stop=False)
                        last = MM(pZ[u % NZB][0:m, r], y[:, 2, n, h * HC + o:h * HC + o + m], mirror[:, :], start=False, stop=True)
                    last.then_inc(s_I, 1)

                def w_in_pair(q):
                    if sW is None:
                        return
                    k, ks, kg = sW
                    if q == 0:
                        need(pe, s_De, k * 2 + 2)
                    need(pe, s_We, k * NPAIR + q)
                    for h in range(2):
                        last = MM(pW[:, h, 0:HC], Xh[ks % 2][:, q * P:(q + 1) * P], wbig[:, h, :], start=True, stop=True)
                    last.then_inc(s_W, 1)

                def transposes(c):
                    if sT is None:
                        return
                    k, ks, kg = sT
                    if c == 0:
                        need(pe, s_xn, k + 1)
                        need(pe, s_De, k * 2)
                        need(pe, s_Oe, (k - L_O) * 2 + 2)
                    else:
                        need(pe, s_Te, k * 2 + 1)
                    for j in range(HP3):
                        q = c * HP3 + j
                        last = nc.tensor.transpose(pX[:, j * P:(j + 1) * P], xn[:, q, :], ident[:, :])
                    last.then_inc(s_T, 1)

                def transform(c):
                    if sT is None:
                        return
                    k, ks, kg = sT
                    if c == 0:
                        need(pe, s_Te, k * 2 + 2)
                    else:
                        need(pe, s_De, k * 2 + 1)
                    for j in range(HP3):
                        q = c * HP3 + j
                        last = MM(pX[:, j * P:(j + 1) * P], xT[:, q * P:(q + 1) * P], cas_s[:, :], start=True, stop=True)
                    last.then_inc(s_D, 1)

                def third_tile(h):
                    if sC is None:
                        return
                    k, ks, kg = sC
                    j = UNITS.index((h, LAST))
                    need(pe, s_st, k + 1)
                    need(pe, s_ca, k * 2)
                    for a, dy, step in ((0, 0, dT), (1, 2, dB)):
                        for dx in range(3):
                            MM(pV[0:MB, h, a * W:(a + 1) * W], dg[:, h, 3 * dy + dx, :], step[0:MB, j, :, dx:dx + T8],
                               start=(dx == 0), stop=(dx == 2))
                    for a, dx, step in ((2, 0, dL), (3, 2, dR)):
                        flat = step[0:MB, j].rearrange("p r j -> p (r j)")
                        for dy in (1, 0, 2):
                            to, fr = max(1 - dy, 0) * NJ, max(dy - 1, 0) * NJ
                            n = (T8 - abs(dy - 1)) * NJ
                            last = MM(pV[0:MB, h, a * W + to:a * W + to + n], dg[:, h, 3 * dy + dx, :], flat[:, fr:fr + n],
                                      start=(dy == 1), stop=(dy == 2))
                    last.then_inc(s_cp, 1)

                def w_out_half(c):
                    if sO is None:
                        return
                    k, ks, kg = sO
                    need(pe, s_m, k * 2 + c + 1)
                    need(pe, s_Oe, k * 2 + c)
                    for i, (_, m) in enumerate(TILE):
                        last = MM(pX[:, 0:HALF], wo[0:m, i, :], z[ks % 2][0:m, 0, i, c * HALF:(c + 1) * HALF],
                                  start=(i == 0), stop=(i == 2))
                    last.then_inc(s_O, 1)

                border_back(0), border_back(1), w_in_pair(0), border_back(2), border_back(3)
                w_in_pair(1), border_back(4), border_back(5), w_out_half(0)
                pixels_back(0, 0), pixels_back(0, 1), w_in_pair(2), w_out_half(1)
                pixels_back(0, 2), pixels_back(0, 3), pixels_back(0, 4), pixels_back(0, 5)
                w_in_pair(3), third_tile(0)
                pixels_back(1, 0), transposes(0), pixels_back(1, 1), w_in_pair(4), third_tile(1)
                pixels_back(1, 2), transposes(1), pixels_back(1, 3), w_in_pair(5), pixels_back(1, 4)
                transform(0), pixels_back(1, 5), transform(1)

            slots(pe, body)

        @block.vector
        def _(dve):
            TT, STT = nc.vector.tensor_tensor, nc.vector.scalar_tensor_tensor
            TC = nc.vector.tensor_copy
            dve.wait_ge(s_c, 16 * NCD)
            for h in range(2):
                TT(dg[:, h], ident[0:MB, 0:MB].unsqueeze(1).broadcast_to([MB, NT, MB]),
                   kt[0:MB, 1, h, :].unsqueeze(2).broadcast_to([MB, NT, MB]), ALU.mult)
            dve.wait_ge(s_sp, 1)
            TC(kT[:, :], pZ[2][0:NT, 0:H2])
            TC(fT[:, :], pZ[1][0:T8 * NF, 0:H2]).then_inc(s_sv, 1)
            for i, (_, m) in enumerate(TILE):
                TC(wo[0:m, i, :], pX[0:m, i * P:(i + 1) * P])
            dve.wait_ge(s_z, NZ0)
            for b in range(IMG):
                r = slice(C * b, C * b + C)
                w = pZ[0][r, 0:H2].rearrange("p (t h) -> p t h", t=2)
                TC(wbig[r, :, b * CA:(b + 1) * CA], w[:, :, 0:CA])
                TC(wbig[r, :, IMG * CA + b * CB:IMG * CA + (b + 1) * CB], w[:, :, CA:HID])
            dve.wait_ge(s_sp, 2)
            TC(fs[:, 0, :], pV[:, 0, 0:H2]).then_inc(s_sv, 1)
            dve.wait_ge(s_sv, 2)
            for i in range(2):
                TT(fs[:, 1 + i, :], fs[:, 0, :], pW[:, i, 0:H2], ALU.mult).then_inc(s_sv, 1)
            dve.wait_ge(s_sv, 4)
            for t in range(NTAB):
                for h in range(2):
                    f = fs[:, t, h * HID:(h + 1) * HID].unsqueeze(1)
                    TC(ftab[:, t, h, 0:IMG * CA].rearrange("p (b c) -> p b c", b=IMG),
                       f[:, :, 0:CA].broadcast_to([P, IMG, CA]))
                    last = TC(ftab[:, t, h, IMG * CA:HC].rearrange("p (b c) -> p b c", b=IMG),
                              f[:, :, CA:HID].broadcast_to([P, IMG, CB]))
            last.then_inc(s_sv, 1)
            dve.wait_ge(s_sv, 5)

            FIX = ([("row", dT, 0, dx) for dx in range(3)] + [("row", dB, 2, dx) for dx in range(3)]
                   + [("col", dL, dy, 0) for dy in range(3)] + [("col", dR, dy, 2) for dy in range(3)])

            def body(strip):
                sW, sC, sO = strip(L_W), strip(L_C), strip(L_O)

                def gate(c):
                    if sO is None:
                        return
                    k, ks, kg = sO
                    need(dve, s_g, k * 2 + c + 1)
                    r = slice(c * HALF, (c + 1) * HALF)
                    TT(z[ks % 2][:, 0, :, r], z[ks % 2][:, 0, :, r], z[ks % 2][:, 1, :, r], ALU.mult).then_inc(s_m, 1)

                def filtered(q):
                    if sW is None:
                        return
                    k, ks, kg = sW
                    need(dve, s_W, k * NPAIR + q + 1)
                    if q == 0:
                        need(dve, s_I, (k - 1) * (2 * NU))
                    if q == HP3:
                        need(dve, s_I, (k - 1) * (2 * NU) + NU)
                    y, n = spectrum(ks, q)
                    for t in range(NTAB):
                        last = TT(y[:, t, n, :].rearrange("p (h c) -> p h c", h=2), pW[:, :, 0:HC], ftab[:, t], ALU.mult)
                    last.then_inc(s_We, 1)

                def steps():
                    if sC is None:
                        return
                    k, ks, kg = sC
                    need(dve, s_Be, k * NU + (2 * NU if ks < NS - 1 else NU))
                    need(dve, s_fx, k * NFIX)
                    need(dve, s_cp, k * 2)
                    own, up, down = bd[ks % 3], bd[(ks - 1) % 3], bd[(ks + 1) % 3]
                    line = lambda t, s, o=0: t[:, :, BOFF + s * BSTR + o:BOFF + s * BSTR + o + W]
                    by_patch = lambda v: v.rearrange("p u (j x) -> p u j x", x=T8)
                    for d, nb, s_nb, s_own, out_of in ((dT, up, 1, 1, ks == 0), (dB, down, 0, 0, ks == NS - 1)):
                        for to, n, own_at in ((1, T8, 0), (0, 1, T8 - 1), (T8 + 1, 1, 0)):
                            o = by_patch(line(own, s_own))[:, :, :, own_at:own_at + n]
                            dst = d[:, :, :, to:to + n]
                            if out_of:
                                last = nc.vector.tensor_scalar(dst, o, -1.0, None, ALU.mult)
                            else:
                                shift = to - 1 - own_at
                                last = TT(dst, by_patch(line(nb, s_nb, shift))[:, :, :, own_at:own_at + n], o, ALU.subtract)
                    for d, s, shift in ((dL, 3, -T8), (dR, 2, T8)):
                        turn = lambda v: by_patch(v).rearrange("p u j x -> p u x j")
                        last = TT(d[:, :, :, :], turn(line(own, s, shift)), turn(line(own, s)), ALU.subtract)
                    last.then_inc(s_st, 1)

                def fix(a, e):
                    if sC is None:
                        return
                    k, ks, kg = sC
                    for n in range(a, e):
                        kind, d, t0, t1 = FIX[n // 2]
                        h = n % 2
                        if n == 0:
                            need(dve, s_Ie, (k + 1) * (2 * NU))
                            need(dve, s_st, k + 1)
                        need(dve, s_fx, k * NFIX + (n - 1))
                        j = UNITS.index((h, 0))
                        zz = z[ks % 2][:, h, 0:2, :]
                        if kind == "row":
                            dy, dx = t0, t1
                            tap = 3 * dy + dx
                            r = 0 if dy == 0 else T8 - 1
                            o = zz[:, :, r * W:(r + 1) * W].rearrange("p i (j x) -> p i j x", x=T8)
                            v = d[:, j:j + 2, :, dx:dx + T8]
                        else:
                            dy, dx = t0, t1
                            tap = 3 * dy + dx
                            to, fr = max(1 - dy, 0) * NJ, max(dy - 1, 0) * NJ
                            m = (T8 - abs(dy - 1)) * NJ
                            x = 0 if dx == 0 else T8 - 1
                            o = zz.rearrange("p i (m x) -> p i m x", x=T8)[:, :, to:to + m, x]
                            v = d[:, j:j + 2].rearrange("p i r j -> p i (r j)")[:, :, fr:fr + m]
                        STT(o, v, kt[:, 0, h, tap:tap + 1], o, ALU.mult, ALU.add).then_inc(s_fx, 1)

                def fix_third():
                    if sC is None:
                        return
                    k, ks, kg = sC
                    zz = z[ks % 2][0:MB, :, LAST, :]
                    need(dve, s_cp, k * 2 + 2)
                    o = zz.rearrange("p h (r w) -> p h r w", r=SR)[:, :, 0:SR:SR - 1, :]
                    TT(o, o, pV[0:MB, :, 0:2 * W].rearrange("p h (r w) -> p h r w", r=2), ALU.add).then_inc(s_ca, 1)
                    need(dve, s_ca, k * 2 + 1)
                    o = zz.rearrange("p h (m x) -> p h x m", x=T8)[:, :, 0:T8:T8 - 1, :]
                    TT(o, o, pV[0:MB, :, 2 * W:4 * W].rearrange("p h (x m) -> p h x m", x=2), ALU.add).then_inc(s_ca, 1)

                def residual(c):
                    if sO is None:
                        return
                    k, ks, kg = sO
                    need(dve, s_O, k * 2 + c + 1)
                    if c == 0:
                        need(dve, s_xr[ks % 2], nth(ks, kg) * 16 + 16)
                    r = slice(c * HALF, (c + 1) * HALF)
                    TT(xr[ks % 2][:, r], pX[:, 0:HALF], xr[ks % 2][:, r], ALU.add).then_inc(s_Oe, 1)

                gate(0), gate(1), filtered(0), filtered(1), residual(0), steps(), filtered(2)
                residual(1), fix(0, 6), filtered(3), fix(6, 12), filtered(4), fix_third(), fix(12, NFIX)
                filtered(5)

            slots(dve, body)


_INS = ["x", "L0_conv_fc0_w", "L0_conv_fc0_b", "L0_conv_fc1_w", "L0_conv_fc1_b", "L0_conv_w1", "L0_conv_b1",
        "L0_conv_w2", "L0_conv_b2", "L1_conv_w_in", "L1_conv_dw_k", "L1_conv_fft_filter", "L1_conv_w_out"]


def build(nc, x, fc0_w, fc0_b, fc1_w, fc1_b, w1, b1, w2, b2, w_in, dw_k, filt, w_out, out):
    x1 = nc.dram_tensor("x1", [G, P, PX], F32, kind="Internal")
    norm2 = nc.dram_tensor("norm2", [G, P, 2], F32, kind="Internal")
    experts_part(nc, x, fc0_w, fc0_b, fc1_w, fc1_b, w1, b1, w2, b2, x1, norm2)
    filter_part(nc, x1, norm2, w_in, dw_k, filt, w_out, out)


def kernel(**inputs):
    import numpy as _np
    import concourse.bacc as _bacc
    from concourse import mybir as _mybir
    from concourse.bass_utils import run_bass_kernel_spmd as _run

    nc = _bacc.Bacc("TRN2", target_bir_lowering=False, num_devices=1)
    arrays, args = {}, []
    for name in _INS:
        a = _np.ascontiguousarray(inputs[name])
        arrays[f"in_{name}_dram"] = a
        args.append(nc.dram_tensor(f"in_{name}_dram", a.shape, _mybir.dt.from_np(a.dtype), kind="ExternalInput").ap())
    out = nc.dram_tensor("out_0_dram", (B, C, H, W), F32, kind="ExternalOutput").ap()
    build(nc, *args, out)
    r = _run(nc, [arrays], core_ids=[0])
    return r.results[0]["out_0_dram"]
```

```python
from contextlib import ExitStack

import numpy as np

import concourse.bass as bass
from concourse import mybir

F32 = mybir.dt.float32
ALU = mybir.AluOpType
ACT = mybir.ActivationFunctionType
AX = mybir.AxisListType

P = 128
B, C, H, W = 32, 32, 96, 96
E, K = 6, 3
IMG = P // C
G = B // IMG
PX = H * W
WP = W + 2
HP = H + 2
TAPS = [(dy, dx) for dy in range(3) for dx in range(3)]
NT = len(TAPS)
GN_EPS = 1e-5

HID = 85
H2 = 2 * HID
T8 = 8
SR = T8
NS = H // SR
NPAIR = W // (2 * T8)
SPX = SR * W
NF = T8 // 2 + 1


def hartley_pairs():
    m = np.arange(T8)
    a = 2 * np.pi * ((m[:, None, None, None] * m[None, None, :, None]
                      + m[None, :, None, None] * m[None, None, None, :]) % T8) / T8
    cas = np.cos(a) + np.sin(a)
    full = np.zeros((T8, 2, T8, 2, T8, T8))
    for j in range(2):
        full[:, j, :, j] = cas
    return full.reshape(P, P).astype(np.float32)


def shift_angles():
    m = np.arange(T8)
    turn = np.array([[[((dy - 1) * u + (dx - 1) * v) % T8 for v in m] for u in m] for dy, dx in TAPS])
    a = 2 * np.pi * turn.reshape(NT, 1, T8 * T8) / T8
    return np.tile(np.concatenate([np.cos(a), np.sin(a)], 1), (1, 1, 2)).astype(np.float32)


def hartley_mirror(cas):
    m = (-np.arange(T8)) % T8
    return cas.reshape(P, 2, T8, T8)[:, :, m][:, :, :, m].reshape(P, P)


def border_columns():
    p = np.arange(P).reshape(T8, 2, T8)
    return np.concatenate([p[0].ravel(), p[-1].ravel(), p[:, :, 0].T.ravel(), p[:, :, -1].T.ravel()])


def filter_spread():
    s = np.zeros((T8, NF, 2, T8, T8))
    for u in range(T8):
        for v in range(T8):
            mu = (-u) % T8
            if v in (0, T8 // 2):
                s[u, v, :, u, v] += 0.5
                s[mu, v, :, u, v] += 0.5
            elif v < T8 // 2:
                s[u, v, :, u, v] = 1.0
            else:
                s[mu, T8 - v, :, u, v] = 1.0
    return s.reshape(T8 * NF, P).astype(np.float32)


CH = 5
R1, R2 = 38, 40
N1, N2 = -(-R1 // CH), R2 // CH
NB1 = 6
BN_ROWS = 4
NBN = H // BN_ROWS

GATE = ["veps", "negm", "rstd", "center", "pool1", "pool2", "pooled", "pmask", "logits", "z", "g", "nabs",
        "exp", "ln", "noise", "nsum", "nmean", "dev", "sq", "ss", "var", "istd", "score", "gt", "eq", "tie",
        "cmp", "rank", "hot", "gp", "gsel", "gmax", "nmax", "cexp", "csum", "crec", "cof", "bcast", "bc",
        "pr0", "pr1", "pr2", "wsel", "w1", "b1", "w2", "cb", "cbs", "bx"]
NG = len(GATE)


def experts_part(nc, x, fc0_w, fc0_b, fc1_w, fc1_b, w1, b1, w2, b2, x1, norm2):
    mask = nc.inline_tensor(np.kron(np.eye(IMG), np.ones((C, 1))).astype(np.float32), name="image_mask")
    mask_t = nc.inline_tensor(np.kron(np.eye(IMG), np.ones((1, C))).astype(np.float32), name="image_mask_t")
    tri_c = nc.inline_tensor(np.tile(np.tril(np.ones((E, E)), -1).reshape(1, E, E), (IMG, 1, 1)).astype(np.float32), name="lower_first")
    slot_c = nc.inline_tensor(np.tile(np.arange(K).reshape(1, K), (IMG, 1)).astype(np.float32), name="slot_numbers")
    eye_c = nc.inline_tensor(np.eye(P, dtype=np.float32), name="eye1")

    xg = x.rearrange("(g b) c h w -> g (b c) h w", b=IMG)
    x1g = x1.ap().rearrange("g p (h w) -> g p h w", h=H)

    with ExitStack() as ctx:
        def sb(name, shape):
            return ctx.enter_context(nc.sbuf_tensor(name, shape, F32))

        def sem(name):
            return ctx.enter_context(nc.semaphore(name))

        X = [sb(f"x_pad{q}", [P, HP, WP]) for q in range(2)]
        Hd = [sb(f"hidden{s}", [P, HP, WP]) for s in range(K)]
        diag = [sb(f"diag{q}", [P, NT, P]) for q in range(2)]
        ident = sb("ident", [P, P])
        wall = sb("wall", [P, E, 20])
        fc = sb("fc", [P, 2 * E])
        fcb = sb("fcb", [IMG, 2 * E])
        m4 = sb("m4", [P, IMG])
        m4t = sb("m4t", [IMG, P])
        tri = sb("tri", [IMG, E, E])
        slots = sb("slots", [IMG, K])
        mhalf = sb("mhalf", [P, 1])
        bn = sb("bn", [P, NBN, 6])
        bn1 = sb("bn1", [P, NBN, 6])
        mv = sb("mv", [P, 2])
        mv1 = sb("mv1", [P, 2])
        col = sb("col", [P, 16])
        v1 = sb("v1", [P, 2])
        st2 = sb("st2", [P, 2])
        row = sb("row", [IMG, 160])
        sq6 = sb("sq6", [IMG, 2, E, E])
        R = sb("R", [IMG, K * E + K])
        bc = sb("bc", [P, K * E + K])
        prod = sb("prod", [P, K, 20, E])
        wsel = sb("wsel", [P, K, 20])
        w1c = [sb(f"w1c{q}", [P, K, NT]) for q in range(2)]
        w2c = [sb(f"w2c{q}", [P, K, NT]) for q in range(2)]
        b1c = [sb(f"b1c{q}", [P, K]) for q in range(2)]
        cb = sb("cb", [P, K + 1])
        bxc = [sb(f"bxc{q}", [P, 1]) for q in range(2)]
        ps = [ctx.enter_context(nc.psum_tensor(f"ps{i}", [P, 512], F32)) for i in range(8)]

        VEPS, NEGM, RSTD, MX, SUMC, P1, P2, PL, PM = 0, 1, 2, 3, 4, 5, 6, 7, 8
        c1 = lambda i, n=1: col[:, i:i + n]
        z, g_, na, ex, ln, noi = (row[:, 12 * i:12 * i + 12] for i in range(6))
        dev, sq, sc, rank = (row[:, 72 + 6 * i:78 + 6 * i] for i in range(4))
        nsum, nmean, ss, var, istd, gmax, nmax, csum, crec = (row[:, 96 + i:97 + i] for i in range(9))
        gsel, cexp = row[:, 106:109], row[:, 110:113]
        gp = row[:, 120:138]

        PE_G = K * N1 + K - 1
        B2_G = NBN + 5
        s_const = sem("const_loaded")
        s_set = sem("buffers_set")
        s_x = [sem(f"x_loaded{q}") for q in range(2)]
        s_st = [sem(f"x1_stored{q}") for q in range(2)]
        s_n2 = sem("norm2_stored")
        s_bns = sem("x_stats")
        s_gate = sem("gate_steps")
        s_diag = sem("diag_built")
        s_pe = sem("pe_units")
        s_c2 = sem("c2_pe_chunks")
        s_ev = sem("c1_pe_evacuated")
        s_tap0 = sem("c1_tap0")
        s_tap1 = sem("c1_taps")
        s_relu = sem("c1_relu")
        s_xb = sem("x_biased")
        s_tap2 = sem("c2_taps")
        s_add = sem("c2_pe_added")
        s_b2 = sem("x1_stats")

        block = ctx.enter_context(nc.Block())
        inner = lambda t, r0, r1: t[:, 1 + r0:1 + r1, 1:1 + W]
        shifted = lambda t, r0, r1, k: t[:, r0 + TAPS[k][0]:r1 + TAPS[k][0], TAPS[k][1]:TAPS[k][1] + W]
        gate_at = lambda g, name: g * NG + GATE.index(name) + 1
        at = lambda g, per, n: g * per + (per + n)
        NCONST = 5 + 7 * IMG + IMG

        def groups(eng, body):
            with eng.Fori(0, G // 2 - 1) as i:
                for q in range(2):
                    body(i * 2 + q, i, q, True)
            for q in range(2):
                body(G - 2 + q, G // 2 - 1, q, q == 0)

        @block.sync
        def _(sp):
            cdma = lambda o, i: sp.dma_start(o, i).then_inc(s_const, 16)
            for q in range(2):
                sp.sem_inc(s_st[q], 16)
            sp.sem_inc(s_n2, 16)
            sp.wait_ge(s_set, 1)
            for h in range(2):
                sp.dma_start(inner(X[0], 48 * h, 48 * h + 48), xg[0][:, 48 * h:48 * h + 48]).then_inc(s_x[0], 16)
            cdma(m4[:, :], mask.ap())
            cdma(m4t[:, :], mask_t.ap())
            cdma(tri[:, :, :], tri_c.ap())
            cdma(slots[:, :], slot_c.ap())
            cdma(ident[:, :], eye_c.ap())
            with nc.allow_non_contiguous_dma(reason="small weight tables, once"):
                for b in range(IMG):
                    o = slice(C * b, C * b + C)
                    cdma(fc[o, 0:E], fc1_w.rearrange("e c -> c e"))
                    cdma(fc[o, E:2 * E], fc0_w.rearrange("e c -> c e"))
                    cdma(wall[o, :, 0:9], w1.rearrange("e c a h w -> c e (a h w)"))
                    cdma(wall[o, :, 9:18], w2.rearrange("e c a h w -> c e (a h w)"))
                    cdma(wall[o, :, 18], b1.rearrange("e c -> c e"))
                    cdma(wall[o, :, 19], b2.rearrange("e c -> c e"))
                    cdma(fcb[b:b + 1, 0:E], fc1_b.rearrange("(a e) -> a e", a=1))
                    cdma(fcb[b:b + 1, E:2 * E], fc0_b.rearrange("(a e) -> a e", a=1))

            def body(g, i, q, more):
                if more:
                    sp.wait_ge(s_set, 2)
                    sp.wait_ge(s_st[1 - q], i * 16 + (16 + 16 * q))
                    for h in range(2):
                        sp.dma_start(inner(X[1 - q], 48 * h, 48 * h + 48),
                                     xg[g + 1][:, 48 * h:48 * h + 48]).then_inc(s_x[1 - q], 16)
                sp.wait_ge(s_add, at(g, N2, N2))
                sp.wait_ge(s_tap2, at(g, K * NT, K * NT))
                sp.dma_start(x1g[g], inner(X[q], 0, H)).then_inc(s_st[q], 16)
                sp.wait_ge(s_b2, at(g, B2_G, B2_G))
                sp.dma_start(norm2.ap()[g], st2[:, :]).then_inc(s_n2, 16)

            groups(sp, body)
            for q in range(2):
                sp.wait_ge(s_st[q], (G // 2 + 1) * 16)
            sp.wait_ge(s_n2, (G + 1) * 16)

        @block.gpsimd
        def _(pool):
            pool.sem_inc(s_diag, 2 * K)
            def clear_border(t):
                nc.gpsimd.memset(t[:, 0, :], 0.0)
                nc.gpsimd.memset(t[:, HP - 1, :], 0.0)
                nc.gpsimd.memset(t[:, 1:HP - 1, 0:1], 0.0)
                nc.gpsimd.memset(t[:, 1:HP - 1, WP - 1:WP], 0.0).then_inc(s_set, 1)

            clear_border(X[0])
            clear_border(X[1])
            nc.gpsimd.memset(mhalf[:, :], -0.5).then_inc(s_set, 1)
            for s in range(K):
                clear_border(Hd[s])
            pool.wait_ge(s_const, 16 * NCONST)
            pool.wait_ge(s_set, 3)

            def rstd(gi):
                pool.wait_ge(s_gate, gate_at(gi, "negm"))
                nc.gpsimd.tensor_tensor(c1(RSTD), c1(VEPS), mhalf[:, :], ALU.pow).then_inc(s_gate, 1)

            def istd_(gi):
                pool.wait_ge(s_gate, gate_at(gi, "var"))
                nc.gpsimd.tensor_tensor(istd, var, mhalf[0:IMG, :], ALU.pow).then_inc(s_gate, 1)

            rstd(0)
            istd_(0)

            def build_diag(g, q, k):
                n = k - 2
                if n == -2:
                    pool.wait_ge(s_gate, g * NG + NG)
                    pool.wait_ge(s_pe, g * PE_G + PE_G)
                elif n == -1:
                    pool.wait_ge(s_c2, g * N2 + N2)
                else:
                    pool.wait_ge(s_pe, at(g, PE_G, (n + 1) * N1 if n < K else K * N1 + n - K + 1))
                wt = (w1c if k < K else w2c)[q][:, k % K, :]
                nc.gpsimd.tensor_tensor(diag[k % 2][:, :, :],
                                        ident[:, :].unsqueeze(1).broadcast_to([P, NT, P]),
                                        wt.unsqueeze(2).broadcast_to([P, NT, P]), ALU.mult).then_inc(s_diag, 1)

            build_diag(0, 0, 0)

            def body(g, i, q, more):
                for k in range(1, 2 * K):
                    build_diag(g, q, k)
                    if k == K and more:
                        rstd(g + 1)
                        istd_(g + 1)
                if more:
                    build_diag(g + 1, 1 - q, 0)
                pool.wait_ge(s_b2, at(g, B2_G, NBN + 2))
                nc.gpsimd.tensor_tensor(v1[:, 1:2], v1[:, 0:1], mhalf[:, :], ALU.pow).then_inc(s_b2, 1)

            groups(pool, body)

        @block.scalar
        def _(act):
            act.sem_inc(s_ev, K * N1)
            act.sem_inc(s_tap0, K)
            act.sem_inc(s_relu, K)
            act.sem_inc(s_xb, 1)

            def center(gi, q):
                act.wait_ge(s_gate, gate_at(gi, "rstd"))
                act.wait_ge(s_bns, gi * (NBN + 2) + (NBN + 2))
                nc.scalar.activation(inner(X[q], 0, H), inner(X[q], 0, H), ACT.Identity,
                                     bias=c1(NEGM), accum_out=c1(SUMC)).then_inc(s_gate, 1)

            def gate_noise(gi):
                act.wait_ge(s_gate, gate_at(gi, "nabs"))
                nc.scalar.activation(ex[:, 0:E], na[:, 0:E], ACT.Exp).then_inc(s_gate, 1)
                act.wait_ge(s_gate, gate_at(gi, "exp"))
                nc.scalar.activation(ln[:, 0:E], ex[:, 0:E], ACT.Ln, bias=1.0).then_inc(s_gate, 1)

            def gate_softmax(gi):
                act.wait_ge(s_gate, gate_at(gi, "nmax"))
                nc.scalar.activation(cexp, gsel, ACT.Exp, bias=nmax).then_inc(s_gate, 1)

            act.wait_ge(s_set, 3 + K)
            center(0, 0)
            gate_noise(0)
            gate_softmax(0)

            def body(g, i, q, more):
                act.wait_ge(s_gate, g * NG + NG)
                for s in range(K):
                    act.wait_ge(s_tap2, g * (K * NT) + (s + 1) * NT)
                    if s < K - 1:
                        act.wait_ge(s_pe, g * PE_G + (K * N1 + s + 1))
                    else:
                        act.wait_ge(s_c2, g * N2 + N2)
                    nc.scalar.activation(inner(Hd[s], R1, H), shifted(X[q], R1, H, 0), ACT.Identity,
                                         scale=w1c[q][:, s, 0:1], bias=b1c[q][:, s:s + 1]).then_inc(s_tap0, 1)
                for s in range(K):
                    for n in range(N1):
                        u = s * N1 + n
                        act.wait_ge(s_pe, at(g, PE_G, u + 1))
                        r0, r1 = n * CH, min(n * CH + CH, R1)
                        nc.scalar.activation(inner(Hd[s], r0, r1),
                                             ps[u % NB1][:, 0:(r1 - r0) * W].rearrange("p (h w) -> p h w", w=W),
                                             ACT.Relu, bias=b1c[q][:, s:s + 1]).then_inc(s_ev, 1)
                        if more and (s, n) == (2, 1):
                            center(g + 1, 1 - q)
                        if more and (s, n) == (2, 6):
                            gate_noise(g + 1)
                            gate_softmax(g + 1)
                    act.wait_ge(s_tap1, at(g, K * (NT - 1), (s + 1) * (NT - 1)))
                    if s == K - 1:
                        nc.scalar.activation(inner(X[q], R2, H), inner(X[q], R2, H), ACT.Identity,
                                             bias=bxc[q][:, :]).then_inc(s_xb, 1)
                    nc.scalar.activation(inner(Hd[s], R1, H), inner(Hd[s], R1, H), ACT.Relu).then_inc(s_relu, 1)

            groups(act, body)

        @block.tensor
        def _(pe):
            pe.sem_inc(s_pe, PE_G)
            pe.sem_inc(s_c2, N2)

            def logits(gi):
                pe.wait_ge(s_gate, gate_at(gi, "pmask"))
                nc.tensor.matmul(ps[7][0:IMG, 0:2 * E], c1(PM, IMG), fc[:, :], start=True, stop=True).then_inc(s_gate, 1)

            def spread(gi):
                pe.wait_ge(s_gate, gate_at(gi, "cof"))
                nc.tensor.matmul(ps[7][:, 0:K * E + K], m4t[:, :], R[:, :], start=True, stop=True).then_inc(s_gate, 1)

            pe.wait_ge(s_const, 16 * NCONST)
            logits(0)
            spread(0)

            def body(g, i, q, more):
                for s in range(K):
                    pe.wait_ge(s_diag, at(g, 2 * K, s + 1))
                    for n in range(N1):
                        u = s * N1 + n
                        if u < NB1:
                            pe.wait_ge(s_add, g * N2 + (u + 1))
                        else:
                            pe.wait_ge(s_ev, at(g, K * N1, u - NB1 + 1))
                        r0, r1 = n * CH, min(n * CH + CH, R1)
                        for k in range(NT):
                            last = nc.tensor.matmul(ps[u % NB1][:, 0:(r1 - r0) * W], diag[s % 2][:, k, :],
                                                    shifted(X[q], r0, r1, k),
                                                    start=(k == 0), stop=(k == NT - 1))
                        last.then_inc(s_pe, 1)
                        if more and (s, n) == (2, 5):
                            pe.wait_ge(s_add, g * N2 + N2)
                            logits(g + 1)
                for s in range(K):
                    pe.wait_ge(s_diag, at(g, 2 * K, K + s + 1))
                    pe.wait_ge(s_ev, at(g, K * N1, K * N1))
                    for n in range(N2):
                        if more and (s, n) == (0, 1):
                            spread(g + 1)
                        if more and (s, n) == (0, N2 - 1):
                            pe.wait_ge(s_gate, gate_at(g + 1, "bc"))
                        if n * CH + CH + 1 > R1 and (n - 1) * CH + CH + 1 <= R1:
                            pe.wait_ge(s_relu, at(g, K, s + 1))
                        for k in range(NT):
                            last = nc.tensor.matmul(ps[n][:, 0:CH * W], diag[(K + s) % 2][:, k, :],
                                                    shifted(Hd[s], n * CH, n * CH + CH, k),
                                                    start=(s == 0 and k == 0), stop=(s == K - 1 and k == NT - 1))
                        if s == K - 1:
                            last.then_inc(s_c2, 1)
                        elif n == N2 - 1:
                            last.then_inc(s_pe, 1)

            groups(pe, body)

        @block.vector
        def _(dve):
            dve.sem_inc(s_tap1, K * (NT - 1))
            dve.sem_inc(s_tap2, K * NT)
            dve.sem_inc(s_add, N2)
            dve.sem_inc(s_b2, B2_G)

            def stats(gi, li, q):
                dve.wait_ge(s_x[q], li * 32 + 32)
                base = gi * (NBN + 2)
                for n in range(NBN):
                    nc.vector.bn_stats(bn[:, n, :], inner(X[q], n * BN_ROWS, (n + 1) * BN_ROWS)).then_inc(s_bns, 1)
                nc.vector.tensor_reduce(c1(MX), inner(X[q], 0, H), axis=AX.XY, op=ALU.max).then_inc(s_bns, 1)
                dve.wait_ge(s_bns, base + NBN)
                nc.vector.tensor_copy(c1(14), m4[:, 0:1])
                nc.vector.bn_aggr(mv[:, :], bn[:, :, :].rearrange("p n s -> p (n s)")).then_inc(s_bns, 1)
                dve.wait_ge(s_bns, base + (NBN + 2))

            def step(gi, name, prev, ins):
                dve.wait_ge(s_gate, gate_at(gi, prev))
                ins().then_inc(s_gate, 1)

            def gate_norm(gi):
                nc.vector.tensor_scalar(c1(VEPS), mv[:, 1:2], GN_EPS, None, ALU.add).then_inc(s_gate, 1)
                nc.vector.tensor_scalar(c1(NEGM), mv[:, 0:1], -1.0, None, ALU.mult).then_inc(s_gate, 1)

            TS, TT, STT = nc.vector.tensor_scalar, nc.vector.tensor_tensor, nc.vector.scalar_tensor_tensor
            RED = nc.vector.tensor_reduce

            def gate_pool(gi):
                step(gi, "pool1", "center", lambda: STT(c1(P1), c1(MX), c1(NEGM), c1(RSTD), ALU.add, ALU.mult))
                step(gi, "pool2", "pool1", lambda: STT(c1(P2), c1(SUMC), 1.0 / PX, c1(RSTD), ALU.mult, ALU.mult))
                step(gi, "pooled", "pool2", lambda: TT(c1(PL), c1(P1), c1(P2), ALU.add))
                step(gi, "pmask", "pooled", lambda: TS(c1(PM, IMG), m4[:, :], c1(PL), None, ALU.mult))

            def gate_choose(gi):
                z0, z6 = z[:, 0:E], z[:, E:2 * E]
                gate, noise, minus = g_[:, 0:E], noi[:, 0:E], na[:, 0:E]
                gt, eq = sq6[:, 0], sq6[:, 1]
                other = lambda t: t.unsqueeze(1).broadcast_to([IMG, E, E])
                own = lambda t: t.unsqueeze(2).broadcast_to([IMG, E, E])
                hot = R[:, 0:K * E].rearrange("p (s e) -> p s e", s=K)
                gp3 = gp.rearrange("p (s e) -> p s e", s=K)
                step(gi, "z", "logits", lambda: TT(z[:, :], ps[7][0:IMG, 0:2 * E], fcb[:, :], ALU.add))
                step(gi, "g", "z", lambda: STT(gate, z0, 0.2, z0, ALU.mult, ALU.max))
                step(gi, "nabs", "z", lambda: STT(minus, z6, -1.0, z6, ALU.mult, ALU.min))
                step(gi, "noise", "ln", lambda: STT(noise, z6, 0.0, ln[:, 0:E], ALU.max, ALU.add))
                step(gi, "nsum", "noise", lambda: RED(nsum, noise, axis=AX.X, op=ALU.add))
                step(gi, "nmean", "nsum", lambda: TS(nmean, nsum, -1.0 / E, None, ALU.mult))
                step(gi, "dev", "nmean", lambda: TS(dev, noise, nmean, None, ALU.add))
                step(gi, "sq", "dev", lambda: TT(sq, dev, dev, ALU.mult))
                step(gi, "ss", "sq", lambda: RED(ss, sq, axis=AX.X, op=ALU.add))
                step(gi, "var", "ss", lambda: TS(var, ss, 1.0 / (E - 1), None, ALU.mult))
                step(gi, "score", "istd", lambda: STT(sc, dev, istd, gate, ALU.mult, ALU.add))
                step(gi, "gt", "score", lambda: TT(gt, other(sc), own(sc), ALU.is_gt))
                step(gi, "eq", "score", lambda: TT(eq, other(sc), own(sc), ALU.is_equal))
                step(gi, "tie", "eq", lambda: TT(eq, eq, tri[:, :, :], ALU.mult))
                step(gi, "cmp", "tie", lambda: TT(gt, gt, eq, ALU.add))
                step(gi, "rank", "cmp", lambda: RED(rank, gt, axis=AX.X, op=ALU.add))
                step(gi, "hot", "rank", lambda: TT(hot, rank.unsqueeze(1).broadcast_to([IMG, K, E]),
                                                   slots[:, :].unsqueeze(2).broadcast_to([IMG, K, E]), ALU.is_equal))
                step(gi, "gp", "hot", lambda: TT(gp3, hot, gate.unsqueeze(1).broadcast_to([IMG, K, E]), ALU.mult))
                step(gi, "gsel", "gp", lambda: RED(gsel, gp3, axis=AX.X, op=ALU.add))
                step(gi, "gmax", "gsel", lambda: RED(gmax, gsel, axis=AX.X, op=ALU.max))
                step(gi, "nmax", "gmax", lambda: TS(nmax, gmax, -1.0, None, ALU.mult))
                step(gi, "csum", "cexp", lambda: RED(csum, cexp, axis=AX.X, op=ALU.add))
                step(gi, "crec", "csum", lambda: nc.vector.reciprocal(crec, csum))
                step(gi, "cof", "crec", lambda: TS(R[:, K * E:K * E + K], cexp, crec, None, ALU.mult))

            def gate_weights(gi, q):
                step(gi, "bc", "bcast", lambda: nc.vector.tensor_copy(bc[:, :], ps[7][:, 0:K * E + K]))
                for s in range(K):
                    step(gi, f"pr{s}", "bc", lambda: TT(
                        prod[:, s], wall[:, :, :].rearrange("p e t -> p t e"),
                        bc[:, s * E:(s + 1) * E].unsqueeze(1).broadcast_to([P, 20, E]), ALU.mult))
                step(gi, "wsel", "pr2", lambda: RED(wsel[:, :, :].rearrange("p s t -> p (s t)"),
                                                    prod[:, :, :, :].rearrange("p s t e -> p (s t) e"),
                                                    axis=AX.X, op=ALU.add))
                cof = bc[:, K * E:K * E + K]
                step(gi, "w1", "wsel", lambda: TS(w1c[q][:, :, :], wsel[:, :, 0:9], c1(RSTD), None, ALU.mult))
                step(gi, "b1", "wsel", lambda: nc.vector.tensor_copy(b1c[q][:, :], wsel[:, :, 18]))
                step(gi, "w2", "wsel", lambda: TT(w2c[q][:, :, :], wsel[:, :, 9:18],
                                                  cof.unsqueeze(2).broadcast_to([P, K, NT]), ALU.mult))
                step(gi, "cb", "wsel", lambda: TT(cb[:, 0:K], wsel[:, :, 19], cof, ALU.mult))
                step(gi, "cbs", "cb", lambda: RED(cb[:, K:K + 1], cb[:, 0:K], axis=AX.X, op=ALU.add))
                step(gi, "bx", "cbs", lambda: TT(bxc[q][:, :], cb[:, K:K + 1], c1(NEGM), ALU.subtract))

            dve.wait_ge(s_const, 16 * NCONST)
            stats(0, 0, 0)
            gate_norm(0)
            gate_pool(0)
            gate_choose(0)
            gate_weights(0, 0)

            def body(g, i, q, more):
                for s in range(K):
                    for k in range(1, NT):
                        if k == 1:
                            dve.wait_ge(s_tap0, at(g, K, s + 1))
                        else:
                            dve.wait_ge(s_tap1, at(g, K * (NT - 1), s * (NT - 1) + k - 1))
                        STT(inner(Hd[s], R1, H), shifted(X[q], R1, H, k), w1c[q][:, s, k:k + 1],
                            inner(Hd[s], R1, H), ALU.mult, ALU.add).then_inc(s_tap1, 1)
                        if more and (s, k) == (1, NT - 1):
                            dve.wait_ge(s_gate, g * NG + NG)
                            stats(g + 1, i + q, 1 - q)
                            gate_norm(g + 1)
                        if more and (s, k) == (2, 3):
                            gate_pool(g + 1)
                        if more and (s, k) == (2, 5):
                            gate_choose(g + 1)
                if more:
                    gate_weights(g + 1, 1 - q)
                dve.wait_ge(s_xb, at(g, 1, 1))
                for s in range(K):
                    dve.wait_ge(s_relu, at(g, K, s + 1))
                    dve.wait_ge(s_ev, at(g, K * N1, (s + 1) * N1))
                    for k in range(NT):
                        if (s, k) != (0, 0):
                            dve.wait_ge(s_tap2, at(g, K * NT, s * NT + k))
                        STT(inner(X[q], R2, H), shifted(Hd[s], R2, H, k), w2c[q][:, s, k:k + 1],
                            inner(X[q], R2, H), ALU.mult, ALU.add).then_inc(s_tap2, 1)
                for n in range(N2):
                    dve.wait_ge(s_c2, at(g, N2, n + 1))
                    r = (n * CH, n * CH + CH)
                    STT(inner(X[q], *r), ps[n][:, 0:CH * W].rearrange("p (h w) -> p h w", h=CH), bxc[q][:, :],
                        inner(X[q], *r), ALU.add, ALU.add).then_inc(s_add, 1)
                dve.wait_ge(s_add, at(g, N2, N2))
                dve.wait_ge(s_tap2, at(g, K * NT, K * NT))
                dve.wait_ge(s_b2, g * B2_G + B2_G)
                for n in range(NBN):
                    nc.vector.bn_stats(bn1[:, n, :], inner(X[q], n * BN_ROWS, (n + 1) * BN_ROWS)).then_inc(s_b2, 1)
                dve.wait_ge(s_b2, at(g, B2_G, NBN))
                nc.vector.tensor_copy(c1(13), m4[:, 0:1])
                nc.vector.bn_aggr(mv1[:, :], bn1[:, :, :].rearrange("p n s -> p (n s)")).then_inc(s_b2, 1)
                dve.wait_ge(s_b2, at(g, B2_G, NBN + 1))
                TS(v1[:, 0:1], mv1[:, 1:2], GN_EPS, None, ALU.add).then_inc(s_b2, 1)
                dve.wait_ge(s_b2, at(g, B2_G, NBN + 3))
                dve.wait_ge(s_n2, g * 16 + 16)
                nc.vector.tensor_copy(st2[:, 0:1], v1[:, 1:2]).then_inc(s_b2, 1)
                STT(st2[:, 1:2], mv1[:, 0:1], -1.0, v1[:, 1:2], ALU.mult, ALU.mult).then_inc(s_b2, 1)

            groups(dve, body)

L_W, L_I, L_C, L_O = 1, 2, 3, 4
HALF = SPX // 2
HP3 = NPAIR // 2
CA = P // 2
CB = HID - CA
HC = IMG * HID
TILE = [(0, P), (P, P), (2 * P, IMG * CB)]
LAST = 2
UNITS = [(1, 0), (1, 1), (1, 2), (0, 0), (0, 1), (0, 2)]
NU = len(UNITS)
NJ = W // T8
NBD = 4 * T8
BSTR = W + 2 * T8
BOFF = T8
BW = BOFF + 4 * BSTR
NTAB = 3
NZB = 3
CKP = 2
NCK = NPAIR // CKP
NIT = NCK * NU
NY = 9
CHAINS = [(0, 0, 2), (0, LAST, 1), (1, 0, 2), (1, LAST, 1)]
NSIDE = 12
NFIX = NSIDE * len(CHAINS)
ORDER = [(2 * h + i, n) for h in range(2) for n in range(NSIDE) for i in range(2)]
NGELU = 2 * NSIDE


def filter_part(nc, x1, norm2, w_in, dw_k, filt, w_out, out):
    cas = hartley_pairs()
    n64 = np.float32(T8 * T8)
    back_n = np.ascontiguousarray(cas.T) / n64
    cas_c = nc.inline_tensor(cas, name="hartley")
    back_c = nc.inline_tensor(back_n, name="hartley_back")
    mirror_c = nc.inline_tensor(np.ascontiguousarray(hartley_mirror(cas).T) / n64, name="hartley_back_mirror")
    border_c = nc.inline_tensor(np.ascontiguousarray(back_n[:, border_columns()]), name="hartley_back_border")
    angle_c = nc.inline_tensor(shift_angles(), name="shift_angles")
    spread_c = nc.inline_tensor(filter_spread(), name="filter_spread")
    eye_c = nc.inline_tensor(np.eye(P, dtype=np.float32), name="eye2")
    og = out.rearrange("(g b) c h w -> g (b c) (h w)", b=IMG)
    x1a, n2a = x1.ap(), norm2.ap()

    with ExitStack() as ctx:
        def sb(name, shape):
            return ctx.enter_context(nc.sbuf_tensor(name, shape, F32))

        def sem(name):
            return ctx.enter_context(nc.semaphore(name))

        xs = [sb(f"x1_strip{i}", [P, SPX]) for i in range(2)]
        xr = [sb(f"x1_again{i}", [P, SPX]) for i in range(2)]
        xn = sb("normed", [P, NPAIR, P])
        xT = sb("pixels_first", [P, SPX])
        Xh = [sb(f"x_spectrum{i}", [P, SPX]) for i in range(2)]
        Y = [sb(f"spectrum{i}", [P, NTAB, 2 * HC]) for i in range(NY)]
        z = [sb(f"hidden_pixels{i}", [P, 2, 3, SPX]) for i in range(2)]
        bd = [sb(f"border{i}", [P, NU, BW]) for i in range(3)]
        dT = sb("step_top", [P, NU, NJ, T8 + 2])
        dB = sb("step_bottom", [P, NU, NJ, T8 + 2])
        dL = sb("step_left", [P, NU, T8, NJ])
        dR = sb("step_right", [P, NU, T8, NJ])
        nrm = sb("norm_scale_bias", [P, 2])
        cas_s, back, mirror, ident = (sb(n, [P, P]) for n in ("cas", "back", "back_mirror", "ident2"))
        border = sb("back_border", [P, 2 * NBD])
        wbig = sb("w_in_by_image", [P, 2, HC])
        ftab = sb("filters", [P, NTAB, 2, HC])
        kt = sb("conv_taps", [P, 2, 2, NT])
        wo = sb("w_out_by_image", [P, 3, P])
        wn = sb("w_in_rows", [HID, 2, IMG, C])
        fn = sb("filter_rows", [HID, 2, T8 * NF])
        kn = sb("tap_rows", [HID, 2, NT])
        fT = sb("filter_t", [T8 * NF, H2])
        kT = sb("taps_t", [NT, H2])
        fs = sb("filters_once", [P, NTAB, H2])
        spr = sb("spread", [T8 * NF, P])
        ang = sb("angles", [NT, 2, P])
        won = sb("w_out_rows", [P, HC])

        pX = ctx.enter_context(nc.psum_tensor("pX", [P, 512], F32))
        pW = ctx.enter_context(nc.psum_tensor("pW", [P, 2, 512], F32))
        pV = ctx.enter_context(nc.psum_tensor("pV", [P, 2, 512], F32))
        pZ = [ctx.enter_context(nc.psum_tensor(f"pZ{i}", [P, 512], F32)) for i in range(NZB)]

        s_c = sem("consts_loaded")
        s_sp = sem("setup_pe")
        s_sv = sem("setup_vector")
        s_z = sem("zeroed")
        s_nrm = sem("norm_loaded")
        s_xs = [sem(f"x1_loaded{i}") for i in range(2)]
        s_xr = [sem(f"x1_again_loaded{i}") for i in range(2)]
        s_os = [sem(f"out_stored{i}") for i in range(2)]
        s_xn = sem("x1_normed")
        s_T = sem("transposed")
        s_Te = sem("transposed_copied")
        s_D = sem("transformed")
        s_De = sem("transformed_copied")
        s_W = sem("w_in_done")
        s_We = sem("filtered")
        s_B = sem("border_back")
        s_Be = sem("border_copied")
        s_I = sem("pixels_back")
        s_Ie = sem("pixels_copied")
        s_st = sem("steps_made")
        s_fx = sem("borders_fixed")
        s_g = sem("gelu_done")
        s_m = sem("gated")
        s_O = sem("w_out_done")
        s_Oe = sem("residual_added")

        block = ctx.enter_context(nc.Block())
        NZ0 = 7
        NCD = 6 + IMG + 2 + 2 + IMG + 2 * IMG + 1
        PEEL = L_O + 2

        def need(eng, s, value):
            if not isinstance(value, int) or value > 0:
                eng.wait_ge(s, value)

        def nth(ks, kg):
            return kg * (NS // 2) + ks // 2

        def slots(eng, body):
            def slot(g, s, last):
                def strip(lag):
                    n = s - lag
                    if (isinstance(g, int) and g == 0 and not last and n < 0) or (last and n >= NS):
                        return None
                    return (g * NS + n, n % NS, g + n // NS)
                body(strip)
            for s in range(PEEL):
                slot(0, s, False)
            with eng.Fori(0, G - 1) as g:
                for s in range(PEEL, PEEL + NS):
                    slot(g, s, False)
            for s in range(PEEL, L_O + NS):
                slot(G - 1, s, True)

        def spectrum(ks, q):
            return Y[(NPAIR * ks + q) % NY]

        @block.sync
        def _(sp):
            cdma = lambda o, i: sp.dma_start(o, i).then_inc(s_c, 16)
            cdma(cas_s[:, :], cas_c.ap())
            cdma(back[:, :], back_c.ap())
            cdma(mirror[:, :], mirror_c.ap())
            cdma(border[:, :], border_c.ap())
            cdma(ident[:, :], eye_c.ap())
            cdma(spr[:, :], spread_c.ap())
            cdma(ang[:, :, :], angle_c.ap())
            with nc.allow_non_contiguous_dma(reason="small weight tables, once"):
                cdma(fn[:, :, :], filt.rearrange("(t h) a e u v -> h t (a e u v)", t=2))
                taps = dw_k.rearrange("(t h) a u v -> h t (a u v)", t=2)
                cdma(kn[:, :, :], taps)
                for b in range(2):
                    cdma(kt[b * CA:b * CA + CA, 0], taps[0:CA])
                for b in range(IMG):
                    cdma(kt[b * CB:b * CB + CB, 1], taps[CA:HID])
                for b in range(IMG):
                    cdma(wn[:, :, b, :], w_in.rearrange("(t h) c -> h t c", t=2))
                sp.wait_ge(s_z, 1)
                for b in range(IMG):
                    r = slice(b * C, b * C + C)
                    cdma(won[r, b * CA:b * CA + CA], w_out[:, 0:CA])
                    cdma(won[r, IMG * CA + b * CB:IMG * CA + b * CB + CB], w_out[:, CA:HID])

            def body(strip):
                if (st := strip(0)) is not None:
                    k, ks, kg = st
                    if ks == 0:
                        need(sp, s_xn, k)
                        sp.dma_start(nrm[:, :], n2a[kg]).then_inc(s_nrm, 16)
                    need(sp, s_xn, k - 1)
                    sp.dma_start(xs[ks % 2][:, :], x1a[kg][:, ks * SPX:(ks + 1) * SPX]).then_inc(s_xs[ks % 2], 16)
                if (st := strip(L_C)) is not None:
                    k, ks, kg = st
                    need(sp, s_os[ks % 2], nth(ks, kg) * 16)
                    sp.dma_start(xr[ks % 2][:, :], x1a[kg][:, ks * SPX:(ks + 1) * SPX]).then_inc(s_xr[ks % 2], 16)
                if (st := strip(L_O)) is not None:
                    k, ks, kg = st
                    need(sp, s_Oe, k * 2 + 2)
                    sp.dma_start(og[kg][:, ks * SPX:(ks + 1) * SPX], xr[ks % 2][:, :]).then_inc(s_os[ks % 2], 16)

            slots(sp, body)
            for i in range(2):
                sp.wait_ge(s_os[i], G * NS // 2 * 16)

        @block.gpsimd
        def _(pool):
            nc.gpsimd.memset(won[:, :], 0.0).then_inc(s_z, 1)
            nc.gpsimd.memset(wbig[:, :, :], 0.0).then_inc(s_z, 1)
            for i in range(3):
                nc.gpsimd.memset(bd[i][:, :, :], 0.0).then_inc(s_z, 1)
            for i in range(2):
                nc.gpsimd.memset(z[i][:, :, :, :], 0.0).then_inc(s_z, 1)

        @block.scalar
        def _(act):
            A = nc.scalar.activation
            act.wait_ge(s_z, NZ0)

            def body(strip):
                sT, sI, sC = strip(0), strip(L_I), strip(L_C)
                def normed():
                    if sT is None:
                        return
                    k, ks, kg = sT
                    need(act, s_xs[ks % 2], nth(ks, kg) * 16 + 16)
                    if ks == 0:
                        need(act, s_nrm, kg * 16 + 16)
                    need(act, s_T, k * 2)
                    A(xn[:, :, :].rearrange("p q (r c) -> p q r c", r=SR),
                      xs[ks % 2][:, :].rearrange("p (r q c) -> p q r c", r=SR, q=NPAIR), ACT.Identity,
                      scale=nrm[:, 0:1], bias=nrm[:, 1:2]).then_inc(s_xn, 1)

                def border_out(j):
                    if sI is None:
                        return
                    k, ks, kg = sI
                    h, i = UNITS[j]
                    m = TILE[i][1]
                    need(act, s_B, k * NU + j + 1)
                    if j == 0:
                        need(act, s_st, k - 1)
                    A(bd[ks % 3][0:m, j, BOFF:BOFF + 4 * BSTR].rearrange("p (s e) -> p s e", s=4)[:, :, 0:W]
                      .rearrange("p s (q c) -> p q s c", q=NPAIR),
                      pV[0:m, j % 2, 0:2 * NBD * NPAIR].rearrange("p (q s c) -> p q s c", q=NPAIR, s=4),
                      ACT.Copy).then_inc(s_Be, 1)

                def pixels_out(c, j):
                    if sI is None:
                        return
                    k, ks, kg = sI
                    h, i = UNITS[j]
                    n, m = c * NU + j, TILE[i][1]
                    need(act, s_I, k * NIT + (n + 1))
                    if n == 0:
                        need(act, s_m, (k - 1) * 2)
                    if (c, h) == (0, 0):
                        need(act, s_O, (k - 1) * 2)
                    A(z[ks % 2][0:m, h, i, :].rearrange("p (r q c) -> p q r c", r=SR, q=NPAIR)[:, c * CKP:(c + 1) * CKP],
                      pZ[n % NZB][0:m, 0:CKP * P].rearrange("p (q r c) -> p q r c", q=CKP, r=SR),
                      ACT.Copy).then_inc(s_Ie, 1)

                def copy(sem_in, sem_out, dst, c):
                    k = sT[0]
                    need(act, sem_in, k * 2 + c + 1)
                    A(dst[:, c * HALF:(c + 1) * HALF], pX[:, 0:HALF], ACT.Copy).then_inc(sem_out, 1)

                for j in range(NU):
                    border_out(j)
                normed()
                for c in range(NCK - 1):
                    for j in range(NU):
                        pixels_out(c, j)
                if sT is not None:
                    need(act, s_D, sT[0] * 2)
                    copy(s_T, s_Te, xT, 0)
                pixels_out(2, 0)
                pixels_out(2, 1)
                if sT is not None:
                    copy(s_T, s_Te, xT, 1)
                pixels_out(2, 2)
                pixels_out(2, 3)
                if sT is not None:
                    need(act, s_W, (sT[0] - 1) * NPAIR)
                    spectra = Xh[sT[1] % 2]
                    copy(s_D, s_De, spectra, 0)
                pixels_out(2, 4)
                if sT is not None:
                    copy(s_D, s_De, spectra, 1)
                pixels_out(2, 5)
                if sC is not None:
                    k, ks, kg = sC
                    need(act, s_fx, k * NFIX + NGELU)
                    for c in range(2):
                        t = z[ks % 2][:, 0, :, c * HALF:(c + 1) * HALF]
                        A(t, t, ACT.Gelu).then_inc(s_g, 1)

            slots(act, body)

        @block.tensor
        def _(pe):
            MM = nc.tensor.matmul
            pe.wait_ge(s_c, 16 * NCD)
            for h in range(2):
                nc.tensor.transpose(pZ[0][:, h * HID:(h + 1) * HID], wn[:, h].rearrange("p b c -> p (b c)"), ident[0:HID, 0:HID])
                nc.tensor.transpose(pZ[1][0:T8 * NF, h * HID:(h + 1) * HID], fn[:, h, :], ident[0:HID, 0:HID])
                nc.tensor.transpose(pZ[2][0:NT, h * HID:(h + 1) * HID], kn[:, h, :], ident[0:HID, 0:HID])
            for i, (o, m) in enumerate(TILE):
                last = nc.tensor.transpose(pX[0:m, i * P:(i + 1) * P], won[:, o:o + m], ident[:, :])
            last.then_inc(s_sp, 1)
            pe.wait_ge(s_sv, 1)
            MM(pV[:, 0, 0:H2], spr[:, :], fT[:, :], start=True, stop=True)
            for i in range(2):
                last = MM(pW[:, i, 0:H2], ang[:, i, :], kT[:, :], start=True, stop=True)
            last.then_inc(s_sp, 1)
            pe.wait_ge(s_sv, 5)

            def body(strip):
                sT, sW, sI, sC, sO = (strip(n) for n in (0, L_W, L_I, L_C, L_O))

                def border_back(j):
                    if sI is None:
                        return
                    k, ks, kg = sI
                    h, i = UNITS[j]
                    o, m = TILE[i]
                    if j == 0:
                        need(pe, s_We, k * NPAIR + NPAIR)
                    need(pe, s_Be, k * NU + (j - 1))
                    for q in range(NPAIR):
                        y = spectrum(ks, q)
                        last = MM(pV[0:m, j % 2, q * 2 * NBD:(q + 1) * 2 * NBD], y[:, 0, h * HC + o:h * HC + o + m],
                                  border[:, :], start=True, stop=True)
                    last.then_inc(s_B, 1)

                def pixels_back(c, j):
                    if sI is None:
                        return
                    k, ks, kg = sI
                    h, i = UNITS[j]
                    o, m = TILE[i]
                    u = c * NU + j
                    need(pe, s_Ie, k * NIT + (u - NZB + 1))
                    for q in range(c * CKP, (c + 1) * CKP):
                        y = spectrum(ks, q)
                        r = slice((q % CKP) * P, (q % CKP + 1) * P)
                        MM(pZ[u % NZB][0:m, r], y[:, 1, h * HC + o:h * HC + o + m], back[:, :], start=True, stop=False)
                        last = MM(pZ[u % NZB][0:m, r], y[:, 2, h * HC + o:h * HC + o + m], mirror[:, :], start=False, stop=True)
                    last.then_inc(s_I, 1)

                def w_in_pair(q):
                    if sW is None:
                        return
                    k, ks, kg = sW
                    if q == 0:
                        need(pe, s_De, k * 2 + 2)
                    need(pe, s_We, k * NPAIR + q)
                    for h in range(2):
                        last = MM(pW[:, h, 0:HC], Xh[ks % 2][:, q * P:(q + 1) * P], wbig[:, h, :], start=True, stop=True)
                    last.then_inc(s_W, 1)

                def transposes(c):
                    if sT is None:
                        return
                    k, ks, kg = sT
                    if c == 0:
                        need(pe, s_xn, k + 1)
                        need(pe, s_De, k * 2)
                        need(pe, s_Oe, (k - L_O) * 2 + 2)
                    else:
                        need(pe, s_Te, k * 2 + 1)
                    for j in range(HP3):
                        q = c * HP3 + j
                        last = nc.tensor.transpose(pX[:, j * P:(j + 1) * P], xn[:, q, :], ident[:, :])
                    last.then_inc(s_T, 1)

                def transform(c):
                    if sT is None:
                        return
                    k, ks, kg = sT
                    if c == 0:
                        need(pe, s_Te, k * 2 + 2)
                    else:
                        need(pe, s_De, k * 2 + 1)
                    for j in range(HP3):
                        q = c * HP3 + j
                        last = MM(pX[:, j * P:(j + 1) * P], xT[:, q * P:(q + 1) * P], cas_s[:, :], start=True, stop=True)
                    last.then_inc(s_D, 1)

                def w_out_half(c):
                    if sO is None:
                        return
                    k, ks, kg = sO
                    need(pe, s_m, k * 2 + c + 1)
                    need(pe, s_Oe, k * 2 + c)
                    for i, (_, m) in enumerate(TILE):
                        last = MM(pX[:, 0:HALF], wo[0:m, i, :], z[ks % 2][0:m, 0, i, c * HALF:(c + 1) * HALF],
                                  start=(i == 0), stop=(i == 2))
                    last.then_inc(s_O, 1)

                w_in_pair(0), border_back(0), border_back(1), border_back(2), w_in_pair(1)
                border_back(3), border_back(4), border_back(5), w_in_pair(2), w_out_half(0)
                pixels_back(0, 0), pixels_back(0, 1), w_out_half(1), pixels_back(0, 2)
                pixels_back(0, 3), pixels_back(0, 4), w_in_pair(3), pixels_back(0, 5)
                pixels_back(1, 0), pixels_back(1, 1), pixels_back(1, 2), w_in_pair(4)
                pixels_back(1, 3), pixels_back(1, 4), pixels_back(1, 5), transposes(0), w_in_pair(5)
                pixels_back(2, 0), transposes(1), pixels_back(2, 1), pixels_back(2, 2)
                pixels_back(2, 3), transform(0), pixels_back(2, 4), transform(1), pixels_back(2, 5)

            slots(pe, body)

        @block.vector
        def _(dve):
            TT, STT = nc.vector.tensor_tensor, nc.vector.scalar_tensor_tensor
            TC = nc.vector.tensor_copy
            dve.wait_ge(s_c, 16 * NCD)
            dve.wait_ge(s_sp, 1)
            TC(kT[:, :], pZ[2][0:NT, 0:H2])
            TC(fT[:, :], pZ[1][0:T8 * NF, 0:H2]).then_inc(s_sv, 1)
            for i, (_, m) in enumerate(TILE):
                TC(wo[0:m, i, :], pX[0:m, i * P:(i + 1) * P])
            dve.wait_ge(s_z, NZ0)
            for b in range(IMG):
                r = slice(C * b, C * b + C)
                w = pZ[0][r, 0:H2].rearrange("p (t h) -> p t h", t=2)
                TC(wbig[r, :, b * CA:(b + 1) * CA], w[:, :, 0:CA])
                TC(wbig[r, :, IMG * CA + b * CB:IMG * CA + (b + 1) * CB], w[:, :, CA:HID])
            dve.wait_ge(s_sp, 2)
            TC(fs[:, 0, :], pV[:, 0, 0:H2]).then_inc(s_sv, 1)
            dve.wait_ge(s_sv, 2)
            for i in range(2):
                TT(fs[:, 1 + i, :], fs[:, 0, :], pW[:, i, 0:H2], ALU.mult).then_inc(s_sv, 1)
            dve.wait_ge(s_sv, 4)
            for t in range(NTAB):
                for h in range(2):
                    f = fs[:, t, h * HID:(h + 1) * HID].unsqueeze(1)
                    TC(ftab[:, t, h, 0:IMG * CA].rearrange("p (b c) -> p b c", b=IMG),
                       f[:, :, 0:CA].broadcast_to([P, IMG, CA]))
                    last = TC(ftab[:, t, h, IMG * CA:HC].rearrange("p (b c) -> p b c", b=IMG),
                              f[:, :, CA:HID].broadcast_to([P, IMG, CB]))
            last.then_inc(s_sv, 1)
            dve.wait_ge(s_sv, 5)

            FIX = ([("row", dT, 0, dx) for dx in range(3)] + [("row", dB, 2, dx) for dx in range(3)]
                   + [("col", dL, dy, 0) for dy in range(3)] + [("col", dR, dy, 2) for dy in range(3)])

            def body(strip):
                sW, sC, sO = strip(L_W), strip(L_C), strip(L_O)

                def gate(c):
                    if sO is None:
                        return
                    k, ks, kg = sO
                    need(dve, s_g, k * 2 + c + 1)
                    need(dve, s_fx, (k + 1) * NFIX)
                    r = slice(c * HALF, (c + 1) * HALF)
                    TT(z[ks % 2][:, 0, :, r], z[ks % 2][:, 0, :, r], z[ks % 2][:, 1, :, r], ALU.mult).then_inc(s_m, 1)

                def filtered(q):
                    if sW is None:
                        return
                    k, ks, kg = sW
                    need(dve, s_W, k * NPAIR + q + 1)
                    if q == 0:
                        need(dve, s_I, (k - 1) * NIT)
                    if q >= NY - NPAIR:
                        need(dve, s_I, (k - 1) * NIT + ((q - (NY - NPAIR)) // CKP + 1) * NU)
                    y = spectrum(ks, q)
                    for t in range(NTAB):
                        last = TT(y[:, t, :].rearrange("p (h c) -> p h c", h=2), pW[:, :, 0:HC], ftab[:, t], ALU.mult)
                    last.then_inc(s_We, 1)

                def steps():
                    if sC is None:
                        return
                    k, ks, kg = sC
                    need(dve, s_Be, k * NU + (2 * NU if ks < NS - 1 else NU))
                    need(dve, s_fx, k * NFIX)
                    own, up, down = bd[ks % 3], bd[(ks - 1) % 3], bd[(ks + 1) % 3]
                    line = lambda t, s, o=0: t[:, :, BOFF + s * BSTR + o:BOFF + s * BSTR + o + W]
                    by_patch = lambda v: v.rearrange("p u (j x) -> p u j x", x=T8)
                    for d, nb, s_nb, s_own, out_of in ((dT, up, 1, 1, ks == 0), (dB, down, 0, 0, ks == NS - 1)):
                        for to, n, own_at in ((1, T8, 0), (0, 1, T8 - 1), (T8 + 1, 1, 0)):
                            o = by_patch(line(own, s_own))[:, :, :, own_at:own_at + n]
                            dst = d[:, :, :, to:to + n]
                            if out_of:
                                last = nc.vector.tensor_scalar(dst, o, -1.0, None, ALU.mult)
                            else:
                                shift = to - 1 - own_at
                                last = TT(dst, by_patch(line(nb, s_nb, shift))[:, :, :, own_at:own_at + n], o, ALU.subtract)
                    for d, s, shift in ((dL, 3, -T8), (dR, 2, T8)):
                        turn = lambda v: by_patch(v).rearrange("p u j x -> p u x j")
                        last = TT(d[:, :, :, :], turn(line(own, s, shift)), turn(line(own, s)), ALU.subtract)
                    last.then_inc(s_st, 1)

                def fix(a, e):
                    if sC is None:
                        return
                    k, ks, kg = sC
                    for n in range(a, e):
                        c, side = ORDER[n]
                        kind, d, dy, dx = FIX[side]
                        h, i, ni = CHAINS[c]
                        m = TILE[i][1]
                        if n == 0:
                            need(dve, s_Ie, (k + 1) * NIT)
                            need(dve, s_st, k + 1)
                        if side > 0:
                            need(dve, s_fx, k * NFIX + (ORDER.index((c, side - 1)) + 1))
                        j = UNITS.index((h, i))
                        zz = z[ks % 2][0:m, h, i:i + ni, :]
                        if kind == "row":
                            r = 0 if dy == 0 else T8 - 1
                            o = zz[:, :, r * W:(r + 1) * W].rearrange("p i (j x) -> p i j x", x=T8)
                            v = d[0:m, j:j + ni, :, dx:dx + T8]
                        else:
                            to, fr = max(1 - dy, 0) * NJ, max(dy - 1, 0) * NJ
                            w = (T8 - abs(dy - 1)) * NJ
                            o = zz.rearrange("p i (m x) -> p i m x", x=T8)[:, :, to:to + w, 0 if dx == 0 else T8 - 1]
                            v = d[0:m, j:j + ni].rearrange("p i r j -> p i (r j)")[:, :, fr:fr + w]
                        tap = 3 * dy + dx
                        STT(o, v, kt[0:m, i // LAST, h, tap:tap + 1], o, ALU.mult, ALU.add).then_inc(s_fx, 1)

                def residual(c):
                    if sO is None:
                        return
                    k, ks, kg = sO
                    need(dve, s_O, k * 2 + c + 1)
                    if c == 0:
                        need(dve, s_xr[ks % 2], nth(ks, kg) * 16 + 16)
                    r = slice(c * HALF, (c + 1) * HALF)
                    TT(xr[ks % 2][:, r], pX[:, 0:HALF], xr[ks % 2][:, r], ALU.add).then_inc(s_Oe, 1)

                filtered(0), gate(0), gate(1), filtered(1), steps(), residual(0), filtered(2)
                fix(0, 8), residual(1), fix(8, 16), filtered(3), fix(16, 24), filtered(4)
                fix(24, 32), filtered(5), fix(32, NFIX)

            slots(dve, body)


_INS = ["x", "L0_conv_fc0_w", "L0_conv_fc0_b", "L0_conv_fc1_w", "L0_conv_fc1_b", "L0_conv_w1", "L0_conv_b1",
        "L0_conv_w2", "L0_conv_b2", "L1_conv_w_in", "L1_conv_dw_k", "L1_conv_fft_filter", "L1_conv_w_out"]


def build(nc, x, fc0_w, fc0_b, fc1_w, fc1_b, w1, b1, w2, b2, w_in, dw_k, filt, w_out, out):
    x1 = nc.dram_tensor("x1", [G, P, PX], F32, kind="Internal")
    norm2 = nc.dram_tensor("norm2", [G, P, 2], F32, kind="Internal")
    experts_part(nc, x, fc0_w, fc0_b, fc1_w, fc1_b, w1, b1, w2, b2, x1, norm2)
    filter_part(nc, x1, norm2, w_in, dw_k, filt, w_out, out)


def kernel(**inputs):
    import numpy as _np
    import concourse.bacc as _bacc
    from concourse import mybir as _mybir
    from concourse.bass_utils import run_bass_kernel_spmd as _run

    nc = _bacc.Bacc("TRN2", target_bir_lowering=False, num_devices=1)
    arrays, args = {}, []
    for name in _INS:
        a = _np.ascontiguousarray(inputs[name])
        arrays[f"in_{name}_dram"] = a
        args.append(nc.dram_tensor(f"in_{name}_dram", a.shape, _mybir.dt.from_np(a.dtype), kind="ExternalInput").ap())
    out = nc.dram_tensor("out_0_dram", (B, C, H, W), F32, kind="ExternalOutput").ap()
    build(nc, *args, out)
    r = _run(nc, [arrays], core_ids=[0])
    return r.results[0]["out_0_dram"]
```
